# Optimizing a Trainium2 kernel written in Bass

```python
import numpy as np
import jax
import jax.numpy as jnp

def _softmax(x, axis=-1):
    return jax.nn.softmax(x, axis=axis)

def _gelu(x):
    return jax.nn.gelu(x, approximate=True)

def _silu(x):
    return jax.nn.silu(x)

def _sigmoid(x):
    return jax.nn.sigmoid(x)

def _layernorm(x, axis=-1, eps=1e-05):
    m = jnp.mean(x, axis=axis, keepdims=True)
    v = jnp.var(x, axis=axis, keepdims=True)
    return (x - m) / jnp.sqrt(v + eps)

def _scatter_add(tgt, idx, src, axis=0):
    return tgt.at[idx].add(src)

def _segment_sum(src, seg, n):
    return jax.ops.segment_sum(src, seg, n)
kernel_name = 'mk_gnn_resnorm_d2_gnn_r32_842d1d'

def setup_inputs(seed: int=0):
    np.random.seed(seed)
    _w = jnp.asarray

    def _rec_inputs():
        import jax
        import jax.numpy as jnp
        _gk = jax.random.key(seed)
        x = -0.0009044 + 1 * jax.random.normal(jax.random.fold_in(_gk, 1), (3125, 16), jnp.float32)
        _s = jax.random.randint(jax.random.fold_in(_gk, 2), (50000,), 0, 3125, jnp.int32)
        _d = jax.random.randint(jax.random.fold_in(_gk, 3), (50000,), 0, 3125, jnp.int32)
        _loop = jnp.arange(3125, dtype=jnp.int32)
        src = jnp.concatenate([_s, _d, _loop])
        dst = jnp.concatenate([_d, _s, _loop])
        _o = jnp.argsort(dst, stable=True)
        src = src[_o]
        dst = dst[_o]
        edge_attr_8 = 0.000398945 + 1.00003 * jax.random.normal(jax.random.fold_in(_gk, 11), (103125, 8), jnp.float32)
        return (x, src, dst, edge_attr_8)
    x, src, dst, edge_attr_8 = _rec_inputs()

    def _L0_gnn_setup():
        import jax, jax.numpy as jnp
        import numpy as np
        N_NODES = 3125
        N_EDGES = 25000
        IN_C = 16
        OUT_C = 16
        EDGE_DIM = 8
        HIDDEN = 64

        def _layernorm(h, w, b, eps=1e-05):
            mu = jnp.mean(h, axis=-1, keepdims=True)
            var = jnp.mean(jnp.square(h - mu), axis=-1, keepdims=True)
            return (h - mu) * jax.lax.rsqrt(var + eps) * w + b
        key = jax.random.key(seed)
        ks = jax.random.split(key, 12)
        x = jax.random.normal(ks[0], (N_NODES, IN_C), dtype=jnp.float32)
        edge_index = jax.random.randint(ks[1], (2, N_EDGES), 0, N_NODES, dtype=jnp.int64)
        edge_attr = jax.random.normal(ks[2], (N_EDGES, EDGE_DIM), dtype=jnp.float32)
        s1 = 1.0 / np.sqrt(EDGE_DIM)
        s2 = 1.0 / np.sqrt(HIDDEN)
        s3 = 1.0 / np.sqrt(IN_C)
        W1 = jax.random.uniform(ks[3], (EDGE_DIM, HIDDEN), jnp.float32, -s1, s1)
        b1 = jax.random.uniform(ks[4], (HIDDEN,), jnp.float32, -s1, s1)
        W2 = jax.random.uniform(ks[5], (HIDDEN, OUT_C * IN_C), jnp.float32, -s2, s2)
        b2 = jax.random.uniform(ks[6], (OUT_C * IN_C,), jnp.float32, -s2, s2)
        root = jax.random.uniform(ks[7], (IN_C, OUT_C), jnp.float32, -s3, s3)
        bias = jnp.zeros((OUT_C,), jnp.float32)
        ln_w = jnp.ones((OUT_C,), jnp.float32)
        ln_b = jnp.zeros((OUT_C,), jnp.float32)
        return {'x': x, 'edge_index': edge_index, 'edge_attr': edge_attr, 'W1': W1, 'b1': b1, 'W2': W2, 'b2': b2, 'root': root, 'bias': bias, 'ln_w': ln_w, 'ln_b': ln_b}
    _L0_gnn_all = _L0_gnn_setup()
    _L0_gnn_in = {k: v for k, v in _L0_gnn_all.items() if k in ('W1', 'b1', 'W2', 'b2', 'root', 'bias', 'ln_w', 'ln_b')}
    del _L0_gnn_all

    def _L1_gnn_setup():
        import jax, jax.numpy as jnp
        import numpy as np
        N_NODES = 6250
        N_EDGES = 100000
        F_IN = 16
        N_CLASSES = 16

        def _gin_conv(x, src, dst, eps, wa, ba, wb, bb, n_nodes):
            agg = jax.ops.segment_sum(x[src], dst, num_segments=n_nodes)
            h = (1.0 + eps) * x + agg
            h = jax.nn.relu(h @ wa + ba) @ wb + bb
            return h
        key = jax.random.key(seed)
        ks = jax.random.split(key, 8)
        s = 1.0 / np.sqrt(F_IN)
        return {'x': jax.random.normal(ks[0], (N_NODES, F_IN), dtype=jnp.float32), 'edge_index': jax.random.randint(ks[1], (2, N_EDGES), 0, N_NODES, dtype=jnp.int32), 'eps1': jnp.zeros((), dtype=jnp.float32), 'w1a': jax.random.normal(ks[2], (F_IN, 16), dtype=jnp.float32) * s, 'b1a': jnp.zeros((16,), dtype=jnp.float32), 'w1b': jax.random.normal(ks[3], (16, 16), dtype=jnp.float32) * 0.25, 'b1b': jnp.zeros((16,), dtype=jnp.float32), 'eps2': jnp.zeros((), dtype=jnp.float32), 'w2a': jax.random.normal(ks[4], (16, N_CLASSES), dtype=jnp.float32) * 0.25, 'b2a': jnp.zeros((N_CLASSES,), dtype=jnp.float32), 'w2b': jax.random.normal(ks[5], (N_CLASSES, N_CLASSES), dtype=jnp.float32) * 0.25, 'b2b': jnp.zeros((N_CLASSES,), dtype=jnp.float32)}
    _L1_gnn_all = _L1_gnn_setup()
    _L1_gnn_in = {k: v for k, v in _L1_gnn_all.items() if k in ('eps1', 'w1a', 'b1a', 'w1b', 'b1b', 'eps2', 'w2a', 'b2a', 'w2b', 'b2b')}
    del _L1_gnn_all
    return {'x': x, 'src': src, 'dst': dst, 'edge_attr_8': edge_attr_8, 'L0_gnn_W1': _L0_gnn_in['W1'], 'L0_gnn_b1': _L0_gnn_in['b1'], 'L0_gnn_W2': _L0_gnn_in['W2'], 'L0_gnn_b2': _L0_gnn_in['b2'], 'L0_gnn_root': _L0_gnn_in['root'], 'L0_gnn_bias': _L0_gnn_in['bias'], 'L0_gnn_ln_w': _L0_gnn_in['ln_w'], 'L0_gnn_ln_b': _L0_gnn_in['ln_b'], 'L1_gnn_eps1': _L1_gnn_in['eps1'], 'L1_gnn_w1a': _L1_gnn_in['w1a'], 'L1_gnn_b1a': _L1_gnn_in['b1a'], 'L1_gnn_w1b': _L1_gnn_in['w1b'], 'L1_gnn_b1b': _L1_gnn_in['b1b'], 'L1_gnn_eps2': _L1_gnn_in['eps2'], 'L1_gnn_w2a': _L1_gnn_in['w2a'], 'L1_gnn_b2a': _L1_gnn_in['b2a'], 'L1_gnn_w2b': _L1_gnn_in['w2b'], 'L1_gnn_b2b': _L1_gnn_in['b2b']}

def reference(x, src, dst, edge_attr_8, L0_gnn_W1, L0_gnn_b1, L0_gnn_W2, L0_gnn_b2, L0_gnn_root, L0_gnn_bias, L0_gnn_ln_w, L0_gnn_ln_b, L1_gnn_eps1, L1_gnn_w1a, L1_gnn_b1a, L1_gnn_w1b, L1_gnn_b1b, L1_gnn_eps2, L1_gnn_w2a, L1_gnn_b2a, L1_gnn_w2b, L1_gnn_b2b):
    import jax
    import jax.numpy as jnp

    def _L0_gnn_ref(x, edge_index, edge_attr, W1, b1, W2, b2, root, bias, ln_w, ln_b):
        import jax, jax.numpy as jnp
        import numpy as np
        N_NODES = 3125
        N_EDGES = 25000
        IN_C = 16
        OUT_C = 16
        EDGE_DIM = 8
        HIDDEN = 64

        def _layernorm(h, w, b, eps=1e-05):
            mu = jnp.mean(h, axis=-1, keepdims=True)
            var = jnp.mean(jnp.square(h - mu), axis=-1, keepdims=True)
            return (h - mu) * jax.lax.rsqrt(var + eps) * w + b
        src = edge_index[0]
        dst = edge_index[1]
        h = jax.nn.silu(edge_attr @ W1 + b1)
        We = (h @ W2 + b2).reshape(-1, IN_C, OUT_C)
        msg = jnp.einsum('ei,eio->eo', x[src], We)
        summed = jax.ops.segment_sum(msg, dst, num_segments=N_NODES)
        cnt = jax.ops.segment_sum(jnp.ones_like(dst, dtype=x.dtype), dst, num_segments=N_NODES)
        aggr = summed / jnp.maximum(cnt, 1.0)[:, None]
        out = aggr + x @ root + bias
        out = _layernorm(out, ln_w, ln_b)
        return jax.nn.silu(out + x)

    def _L1_gnn_ref(x, edge_index, eps1, w1a, b1a, w1b, b1b, eps2, w2a, b2a, w2b, b2b):
        import jax, jax.numpy as jnp
        import numpy as np
        N_NODES = 6250
        N_EDGES = 100000
        F_IN = 16
        N_CLASSES = 16

        def _gin_conv(x, src, dst, eps, wa, ba, wb, bb, n_nodes):
            agg = jax.ops.segment_sum(x[src], dst, num_segments=n_nodes)
            h = (1.0 + eps) * x + agg
            h = jax.nn.relu(h @ wa + ba) @ wb + bb
            return h
        src, dst = (edge_index[0], edge_index[1])
        n = x.shape[0]
        h = jax.nn.relu(_gin_conv(x, src, dst, eps1, w1a, b1a, w1b, b1b, n))
        h = _gin_conv(h, src, dst, eps2, w2a, b2a, w2b, b2b, n)
        return jax.nn.log_softmax(h, axis=1)
    edge_index = jnp.stack([src, dst])
    x = _layernorm(x + _L0_gnn_ref(x, edge_index, edge_attr_8, L0_gnn_W1, L0_gnn_b1, L0_gnn_W2, L0_gnn_b2, L0_gnn_root, L0_gnn_bias, L0_gnn_ln_w, L0_gnn_ln_b), axis=-1)
    x = _layernorm(x + _L1_gnn_ref(x, edge_index, L1_gnn_eps1, L1_gnn_w1a, L1_gnn_b1a, L1_gnn_w1b, L1_gnn_b1b, L1_gnn_eps2, L1_gnn_w2a, L1_gnn_b2a, L1_gnn_w2b, L1_gnn_b2b), axis=-1)
    return x

_drawn_inputs = setup_inputs


def setup_inputs(seed=0):
    import zlib

    import numpy as np

    out = dict(_drawn_inputs(seed))
    spreads = {'L0_gnn_bias': (0.0, 0.1),
     'L0_gnn_ln_w': (1.0, 0.2),
     'L0_gnn_ln_b': (0.0, 0.1),
     'L1_gnn_b1a': (0.0, 0.8),
     'L1_gnn_b1b': (0.0, 0.275),
     'L1_gnn_b2a': (0.0, 2.0),
     'L1_gnn_b2b': (0.0, 2.0)}
    factors = {'L0_gnn_b1': 3.891, 'L0_gnn_b2': 2.825}
    for name, (base, spread) in spreads.items():
        noise = np.random.default_rng([zlib.crc32(name.encode()), seed]).standard_normal(out[name].shape)
        drawn = base * np.exp(spread * noise) if base else spread * noise
        out[name] = jnp.asarray(drawn.astype(out[name].dtype))
    for name, factor in factors.items():
        out[name] = (out[name] * factor).astype(out[name].dtype)
    return out
```

```python
import concourse.bass as bass
from concourse import mybir
from contextlib import ExitStack

NODES, F, EDGES = 3125, 16, 103125
EDGE_F, HIDDEN = 8, 64
P = 128
H = P // F
L = -(-NODES // H)
LP = L + L % 2
TILES = 8
GROUPS = -(-EDGES // (P * TILES))
PAIRS = GROUPS // 2
CHUNKS = [(c, min(P, L - c)) for c in range(0, L, P)]
SPLITS = 3
VECS = ["bias", "ln_w", "ln_b", "b1a", "b1b", "b2a", "eps1", "eps2"]
MATS = ["root", "B2", "w1a", "w1b", "w2a", "w2b", "mean"]
EPS = 1e-5
assert GROUPS == 2 * PAIRS + 1


def gnn_kernel(nc, x_rows, x_cols, ids, edge_attr, w1, b1, w2, mats, vecs, b2b_row, ident, iotas, out):
    f32, bf16, f16, i32 = mybir.dt.float32, mybir.dt.bfloat16, mybir.dt.float16, mybir.dt.int32
    ALU, ACT, AX = mybir.AluOpType, mybir.ActivationFunctionType, mybir.AxisListType

    ctx = ExitStack()
    with ctx:
        def sb(name, shape, dt):
            return ctx.enter_context(nc.sbuf_tensor(name, shape, dt))

        def ps(name, shape, dt=f32):
            return ctx.enter_context(nc.psum_tensor(name, shape, dt))

        def sem(name):
            return ctx.enter_context(nc.semaphore(name))

        table_xy = nc.dram_tensor("table_xy", (L * H, 2 * F), f32, kind="Internal").ap()
        table_x1 = nc.dram_tensor("table_x1", (L * H, F), f32, kind="Internal").ap()
        table_h1 = nc.dram_tensor("table_h1", (L * H, F), f32, kind="Internal").ap()

        w1_sb = sb("w1_sb", [2 * EDGE_F, P], f32)
        b1_sb = sb("b1_sb", [P, 1], f32)
        w2_sb = sb("w2_sb", [P, F * F], f32)
        mats_sb = sb("mats_sb", [P, len(MATS), P], f32)
        vecs_sb = sb("vecs_sb", [P, len(VECS)], f32)
        b2b_sb = sb("b2b_sb", [P, P], f32)
        ident_sb = sb("ident_sb", [P, P], f32)
        iota_sb = sb("iota_sb", [P, H + LP], f32)
        iota_h = sb("iota_h", [P, H], f32)
        iota_l = sb("iota_l", [P, LP], f16)
        zero_sb = sb("zero_sb", [P, L], bf16)
        mat = {n: mats_sb[:, k, :] for k, n in enumerate(MATS)}
        vec = {n: vecs_sb[:, k:k + 1] for k, n in enumerate(VECS)}

        ids_sb = [sb(f"ids{s}", [P, 2 * TILES], i32) for s in range(2)]
        ea_sb = [sb(f"ea{s}", [2 * EDGE_F, P * TILES // 2], f32) for s in range(2)]
        hid_sb = [sb(f"hid{s}", [P, P * TILES // 2], f32) for s in range(2)]
        rows_xy = [sb(f"rows_xy{s}", [P, TILES, 2 * F], f32) for s in range(2)]
        rows_x = [sb(f"rows_x{s}", [P, TILES, F], f32) for s in range(2)]
        dst_h = sb("dst_h", [P, TILES], i32)
        dst_l = sb("dst_l", [P, TILES], i32)
        dst_hf = sb("dst_hf", [P, TILES], f32)
        dst_lf = sb("dst_lf", [P, TILES], f32)
        hot_h = [sb(f"hot_h{s}", [P, TILES, H], bf16) for s in range(2)]
        hot_l = [sb(f"hot_l{s}", [P, TILES, LP], bf16) for s in range(2)]
        prod = [sb(f"prod{q}", [P, 4, F, F], f32) for q in range(2)]
        msg = sb("msg", [P, TILES, F], f32)
        rest1 = sb("rest1", [P, TILES, F], f32)
        rest2 = sb("rest2", [P, TILES, F], f32)
        part = [sb(f"part{k}", [P, TILES, F], bf16) for k in range(SPLITS)]
        spread = [sb(f"spread{s}", [P, SPLITS, TILES, H, F], bf16) for s in range(2)]

        x_row = sb("x_row", [P, 4, H, F], f32)
        xy_row = sb("xy_row", [P, 4, H, 2, F], f32)
        x_col = sb("x_col", [P, L], f32)
        x1_col = sb("x1_col", [P, L], f32)
        x1_row = sb("x1_row", [P, 4, P], f32)
        h1_col = sb("h1_col", [P, L], f32)
        h1_row = sb("h1_row", [P, 4, P], f32)
        ta = sb("ta", [P, L], f32)
        tb = sb("tb", [P, L], f32)
        tc = sb("tc", [P, L], f32)
        rcnt = sb("rcnt", [H, L], f32)
        rep = sb("rep", [H, P], f32)
        y = sb("y", [P, 4 * H, F], f32)
        y2 = sb("y2", [P, 4 * H, F], f32)
        red = sb("red", [P, 4 * H], f32)
        red2 = sb("red2", [P, 4 * H], f32)

        acc = ps("acc", [P, 512])
        cnt = ps("cnt", [P, 512])
        hid_ps = ps("hid_ps", [P, 512])
        we_ps = ps("we_ps", [P, 4, 512])
        node_ps = ps("node_ps", [P, 512])

        consts_in = sem("consts_in")
        x_in = sem("x_in")
        consts_ready = sem("consts_ready")
        table_in = sem("table_in")
        v_done = sem("v_done")
        a_done = sem("a_done")
        p_done = sem("p_done")
        out_done = sem("out_done")

        class Edges:
            def __init__(self, name, mlp):
                self.mlp = mlp
                self.ids_in = [sem(f"{name}_ids_in{s}") for s in range(2)]
                self.ids_used = [sem(f"{name}_ids_used{s}") for s in range(2)]
                self.ea_in = [sem(f"{name}_ea_in{s}") for s in range(2)]
                self.hid_made = sem(f"{name}_hid_made")
                self.hid_read = sem(f"{name}_hid_read")
                self.silu = [sem(f"{name}_silu{s}") for s in range(2)]
                self.we_made = [[sem(f"{name}_we_made{q}{s}") for s in range(2)] for q in range(2)]
                self.we_read = [sem(f"{name}_we_read{q}") for q in range(2)]
                self.turns = sem(f"{name}_turns")
                self.rows_in = [sem(f"{name}_rows_in{s}") for s in range(2)]
                self.rows_used = [sem(f"{name}_rows_used{s}") for s in range(2)]
                self.hots = [sem(f"{name}_hots{s}") for s in range(2)]
                self.spreads = [sem(f"{name}_spreads{s}") for s in range(2)]
                self.scattered = [sem(f"{name}_scattered{s}") for s in range(2)]
                self.vec = sem(f"{name}_vec")
                self.summed = sem(f"{name}_summed")

        conv = Edges("conv", True)
        gin1 = Edges("gin1", False)
        gin2 = Edges("gin2", False)

        def pairs(eng, step, first=0, last=PAIRS):
            with eng.Fori(first, last) as i:
                for s in range(2):
                    step(2 * i + s, i, s)

        block = ctx.enter_context(nc.Block())

        @block.sync
        def _(sp):
            for c, n in CHUNKS:
                sp.dma_start(x_row[0:n, c // P, :, :], x_rows[c:c + n, :].rearrange("l (h f) -> l h f", f=F)).then_inc(x_in, 16)
            sp.dma_start(x_col[:, :], x_cols).then_inc(x_in, 16)
            sp.dma_start(mats_sb[:, :, :], mats).then_inc(x_in, 16)
            for dst, src in ((w1_sb, w1), (b1_sb, b1), (w2_sb, w2), (vecs_sb, vecs), (b2b_sb, b2b_row),
                             (ident_sb, ident), (iota_sb, iotas)):
                sp.dma_start(dst[:, :], src).then_inc(consts_in, 16)

            def write_table(table, rows, width):
                for c, n in CHUNKS:
                    sp.dma_start(table.rearrange("(l h) f -> l (h f)", h=H)[c:c + n, :],
                                 rows[0:n, c // P, :]).then_inc(table_in, 16)

            def feed(e):
                def load(g, i, s, fresh=False):
                    if not fresh:
                        sp.wait_ge(e.rows_in[s], 16 * TILES * i)
                        sp.wait_ge(e.ids_used[s], i)
                    sp.dma_start(ids_sb[s][:, :], ids[bass.ds(g, 1), :, :].rearrange("o p n -> p (o n)")).then_inc(e.ids_in[s], 16)
                    if e.mlp:
                        if not fresh:
                            sp.wait_ge(e.silu[s], i)
                        sp.dma_start(ea_sb[s][:, :], edge_attr[bass.ds(g, 1), :, :].rearrange("o k n -> k (o n)")).then_inc(e.ea_in[s], 16)
                for g in range(2):
                    load(g, 0, g, fresh=True)
                pairs(sp, load, first=1)
                load(GROUPS - 1, PAIRS, 0)

            sp.wait_ge(v_done, V["xy"])
            write_table(table_xy, xy_row[:, :, :, :, :].rearrange("p c h t f -> p c (h t f)"), 2 * F)
            feed(conv)
            sp.wait_ge(v_done, V["x1_row"])
            write_table(table_x1, x1_row, F)
            feed(gin1)
            sp.wait_ge(v_done, V["h1_row"])
            write_table(table_h1, h1_row, F)
            feed(gin2)
            sp.wait_ge(v_done, V["out"])
            y_rows = y[:, :, :].rearrange("p (c h) f -> p c (h f)", h=H)
            o_flat = out.rearrange("n f -> (n f)")
            full = NODES // H
            for c, n in CHUNKS:
                m = min(n, full - c)
                sp.dma_start(o_flat[c * P:(c + m) * P].rearrange("(l k) -> l k", k=P), y_rows[0:m, c // P, :]).then_inc(out_done, 16)
            tail = (NODES - full * H) * F
            c, m = CHUNKS[-1][0], full - CHUNKS[-1][0]
            sp.dma_start(o_flat[full * P:NODES * F].rearrange("(o k) -> o k", o=1), y_rows[m:m + 1, c // P, 0:tail]).then_inc(out_done, 16)
            sp.wait_ge(out_done, 16 * (len(CHUNKS) + 1))

        @block.gpsimd
        def _(pool):
            def gather(e, table, rows):
                def step(g, i, s):
                    pool.wait_ge(e.ids_in[s], 16 * (i + 1))
                    pool.wait_ge(e.rows_used[s], i + 1)
                    pool.sem_inc(e.turns, 1)
                    for t in range(TILES):
                        pool.indirect_dma_start(
                            out=rows[s][:, t, :], out_offset=None, in_=table,
                            in_offset=bass.IndirectOffsetOnAxis(ap=ids_sb[s][:, t:t + 1], axis=0),
                        ).then_inc(e.rows_in[s], 16)
                pairs(pool, step)
                step(GROUPS - 1, PAIRS, 0)

            n_table = 16 * len(CHUNKS)
            pool.wait_ge(table_in, n_table)
            gather(conv, table_xy, rows_xy)
            pool.wait_ge(table_in, 2 * n_table)
            gather(gin1, table_x1, rows_x)
            pool.wait_ge(table_in, 3 * n_table)
            gather(gin2, table_h1, rows_x)

        @block.tensor
        def _(pe):
            for e in (conv, gin1, gin2):
                for s in range(2):
                    pe.sem_inc(e.scattered[s], 1)
            for q in range(2):
                for s in range(2):
                    pe.sem_inc(conv.we_made[q][s], 1)
            def scatter(e, i, s):
                pe.wait_ge(e.hots[s], i + 1)
                pe.wait_ge(e.spreads[s], i + 1)
                for t in range(TILES):
                    for k in range(SPLITS):
                        mm = pe.matmul(acc[:, 0:L], spread[s][:, k, t, :, :].rearrange("p h f -> p (h f)"),
                                       hot_l[s][:, t, 0:L], start=False, stop=False, skip_group_check=True)
                    if e.mlp:
                        mm = pe.matmul(cnt[0:H, 0:L], hot_h[s][:, t, :], hot_l[s][:, t, 0:L],
                                       start=False, stop=False, skip_group_check=True)
                mm.then_inc(e.scattered[s], 1)

            def open_sums(e):
                pe.matmul(acc[:, 0:L], zero_sb[:, 0:P], zero_sb[:, :], start=True, stop=False, skip_group_check=True)
                if e.mlp:
                    pe.matmul(cnt[0:H, 0:L], zero_sb[:, 0:H], zero_sb[:, :], start=True, stop=False, skip_group_check=True)

            def close_sums(e):
                mm = pe.matmul(acc[:, 0:L], zero_sb[:, 0:P], zero_sb[:, :], start=False, stop=True, skip_group_check=True)
                if e.mlp:
                    mm = pe.matmul(cnt[0:H, 0:L], zero_sb[:, 0:H], zero_sb[:, :], start=False, stop=True, skip_group_check=True)
                mm.then_inc(e.summed, 1)

            def hidden(g, i, s):
                pe.wait_ge(conv.ea_in[s], 16 * (i + 1))
                pe.wait_ge(conv.hid_read, g + 1)
                pe.matmul(hid_ps[:, :], w1_sb[:, :], ea_sb[s][:, :], start=True, stop=True).then_inc(conv.hid_made, 1)

            def edge_weights(g, i, s):
                pe.wait_ge(conv.silu[s], i + 1)
                for q in range(2):
                    pe.wait_ge(conv.we_read[q], g + 1)
                    for k in range(2):
                        for half in range(2):
                            t = 4 * q + 2 * half + k
                            rows = slice(64 * half, 64 * half + 64)
                            col = P * (2 * q + k)
                            mm = pe.matmul(we_ps[:, 2 * q + half, 256 * k:256 * k + 256],
                                           hid_sb[s][rows, col:col + P], w2_sb[rows, :], start=True, stop=True)
                    mm.then_inc(conv.we_made[q][s], 1)
                    if q:
                        pass

            pe.wait_ge(x_in, 16 * (len(CHUNKS) + 2))
            for c, n in CHUNKS:
                mm = pe.matmul(node_ps[0:n, c:c + P], x_col[:, c:c + n], mat["B2"], start=True, stop=True)
            mm.then_inc(p_done, 1)
            pe.wait_ge(consts_ready, 1)
            open_sums(conv)

            def conv_step(g, i, s):
                hidden(g, i, s)
                scatter(conv, i - 1, s)
                edge_weights(g, i, s)

            for g in range(2):
                hidden(g, 0, g)
                edge_weights(g, 0, g)
            pairs(pe, conv_step, first=1)
            conv_step(GROUPS - 1, PAIRS, 0)
            scatter(conv, PAIRS - 1, 1)
            scatter(conv, PAIRS, 0)
            close_sums(conv)

            def cols(dst, weights, src, v):
                pe.wait_ge(v_done, v)
                pe.matmul(dst, weights, src, start=True, stop=True).then_inc(p_done, 1)

            def acols(dst, weights, src, a):
                pe.wait_ge(a_done, a)
                pe.matmul(dst, weights, src, start=True, stop=True).then_inc(p_done, 1)

            def to_rows(dst, src, v):
                pe.wait_ge(v_done, v)
                for c, n in CHUNKS:
                    mm = pe.transpose(dst[0:n, c:c + P], src[:, c:c + n], ident_sb[:, :])
                mm.then_inc(p_done, 1)

            node, big = node_ps[:, 0:L], hid_ps[:, 0:L]
            cols(node, rep[:, :], rcnt[:, :], V["rcnt"])
            pe.matmul(big, mat["root"], x_col[:, :], start=True, stop=True).then_inc(p_done, 1)
            cols(node, mat["mean"], ta[:, :], V["conv_out"])
            cols(node, mat["mean"], tc[:, :], V["conv_sq"])
            cols(node, mat["mean"], ta[:, :], V["res1"])
            cols(node, mat["mean"], tc[:, :], V["res1_sq"])
            to_rows(node_ps, x1_col, V["x1"])

            def gin(e):
                open_sums(e)
                pairs(pe, lambda g, i, s: scatter(e, i, s))
                scatter(e, PAIRS, 0)
                close_sums(e)

            gin(gin1)
            cols(node, mat["w1a"], ta[:, :], V["gin1_in"])
            acols(big, mat["w1b"], tb[:, :], A["gin1_mid"])
            to_rows(node_ps, h1_col, V["h1"])
            gin(gin2)
            cols(node, mat["w2a"], ta[:, :], V["gin2_in"])
            pe.wait_ge(a_done, A["gin2_mid"])
            for c, n in CHUNKS:
                mm = pe.matmul(hid_ps[0:n, c:c + P], tb[:, c:c + n], mat["w2b"], start=True, stop=True)
            mm.then_inc(p_done, 1)

        @block.scalar
        def _(act):
            act.sem_inc(conv.hid_read, 1)
            act.wait_ge(consts_ready, 1)

            def silu(g, i, s):
                act.wait_ge(conv.hid_made, g + 1)
                act.wait_ge(conv.we_made[1][s], i + 1)
                act.activation(hid_sb[s][:, :], hid_ps[:, :], ACT.Silu, bias=b1_sb[:, 0:1]).then_inc(conv.silu[s], 1)
                act.wait_ge(conv.silu[s], i + 1)
                act.sem_inc(conv.hid_read, 1)
            pairs(act, silu)
            silu(GROUPS - 1, PAIRS, 0)

            def one(v, dst, src, fn, **kw):
                act.wait_ge(v_done, v)
                act.activation(dst, src, fn, **kw).then_inc(a_done, 1)
            one(V["conv_var"], tc[:, :], tb[:, :], ACT.Sqrt)
            one(V["conv_pre"], tb[:, :], ta[:, :], ACT.Silu)
            one(V["res1_var"], tc[:, :], tb[:, :], ACT.Sqrt)
            act.wait_ge(p_done, PD["gin1_a"])
            act.activation(tb[:, :], node_ps[:, 0:L], ACT.Relu, bias=vec["b1a"]).then_inc(a_done, 1)
            act.wait_ge(p_done, PD["gin1_b"])
            act.activation(h1_col[:, :], hid_ps[:, 0:L], ACT.Relu, bias=vec["b1b"]).then_inc(a_done, 1)
            act.wait_ge(p_done, PD["gin2_a"])
            act.activation(tb[:, :], node_ps[:, 0:L], ACT.Relu, bias=vec["b2a"]).then_inc(a_done, 1)
            one(V["shifted"], y2[:, :, :], y[:, :, :], ACT.Exp)
            one(V["expsum"], red2[:, :], red[:, :], ACT.Ln)
            one(V["out_var"], red2[:, :], red[:, :], ACT.Sqrt)

        @block.vector
        def _(dve):
            state = {"v": 0}

            def done(ins, name=None):
                state["v"] += 1
                ins.then_inc(v_done, 1)
                if name:
                    assert V[name] == state["v"], (name, state["v"])

            def after():
                dve.wait_ge(v_done, state["v"])

            for e in (conv, gin1, gin2):
                for s in range(2):
                    dve.sem_inc(e.rows_used[s], 1)
            for q in range(2):
                dve.sem_inc(conv.we_read[q], 1)
            dve.wait_ge(consts_in, 16 * 7)
            dve.wait_ge(x_in, 16 * (len(CHUNKS) + 2))
            dve.tensor_copy(iota_h[:, :], iota_sb[:, 0:H])
            dve.memset(zero_sb[:, :], 0.0)
            dve.memset(xy_row[:, 3, :, :, :], 0.0)
            dve.memset(y[:, :, :], 0.0)
            dve.memset(x1_row[:, 3, :], 0.0)
            done(dve.tensor_copy(rep[:, :].rearrange("k (h f) -> k h f", f=F),
                                 ident_sb[0:H, 0:H].unsqueeze(2).to_broadcast([H, H, F])), "rep")
            dve.tensor_copy(iota_l[:, :], iota_sb[:, H:H + LP]).then_inc(consts_ready, 1)
            after()
            for c, n in CHUNKS:
                done(dve.tensor_copy(xy_row[0:n, c // P, :, 0, :], x_row[0:n, c // P, :, :]))
            dve.wait_ge(p_done, PD["xB2"])
            for c, n in CHUNKS:
                done(dve.tensor_copy(xy_row[0:n, c // P, :, 1, :],
                                     node_ps[0:n, c:c + P].rearrange("p (h f) -> p h f", f=F)),
                     "xy" if c == CHUNKS[-1][0] else None)
            dve.wait_ge(consts_ready, 1)

            def edge_pass(e, rows):
                per = 10 if e.mlp else 7

                def step(g, i, s):
                    at = {"n": 0}

                    def chain(ins):
                        at["n"] += 1
                        ins.then_inc(e.vec, 1)

                    def chained(back=0):
                        dve.wait_ge(e.vec, per * g + at["n"] - back)

                    dve.wait_ge(e.ids_in[s], 16 * (i + 1))
                    dve.wait_ge(e.scattered[s], i + 1)
                    dve.tensor_scalar(dst_h[:, :], ids_sb[s][:, TILES:], H - 1, None, ALU.bitwise_and)
                    chain(dve.tensor_scalar(dst_l[:, :], ids_sb[s][:, TILES:], 3, None, ALU.logical_shift_right))
                    chained()
                    dve.tensor_copy(dst_hf[:, :], dst_h[:, :])
                    chain(dve.tensor_copy(dst_lf[:, :], dst_l[:, :]))
                    chained()
                    dve.tensor_tensor(hot_h[s][:, :, :], dst_hf[:, :].unsqueeze(2).to_broadcast([P, TILES, H]),
                                      iota_h[:, :].unsqueeze(1).to_broadcast([P, TILES, H]), ALU.is_equal).then_inc(e.ids_used[s], 1)
                    for t in range(TILES):
                        ins = dve.tensor_scalar(hot_l[s][:, t, :], iota_l[:, :], dst_lf[:, t:t + 1], None, ALU.is_equal)
                    ins.then_inc(e.hots[s], 1)
                    dve.wait_ge(e.rows_in[s], 16 * TILES * (i + 1))
                    if e.mlp:
                        for q in range(2):
                            dve.wait_ge(e.we_made[q][s], i + 2)
                            weights = we_ps[:, 2 * q:2 * q + 2, :].rearrange("p b (k o i) -> p (b k) o i", k=2, o=F)
                            x_in_edge = rows[s][:, 4 * q:4 * q + 4, 0:F].unsqueeze(2).to_broadcast([P, 4, F, F])
                            dve.tensor_tensor(prod[q][:, :, :, :], weights, x_in_edge, ALU.mult).then_inc(e.we_read[q], 1)
                            dve.wait_ge(e.we_read[q], g + 2)
                            chain(dve.tensor_reduce(msg[:, 4 * q:4 * q + 4, :], prod[q][:, :, :, :], AX.X, ALU.add))
                        chained()
                        chain(dve.tensor_tensor(msg[:, :, :], msg[:, :, :], rows[s][:, :, F:2 * F], ALU.add))
                        chained()
                        dve.sem_inc(e.rows_used[s], 1)
                        value = msg
                    else:
                        value = rows[s]
                    chain(dve.tensor_copy(part[0][:, :, :], value[:, :, :]))
                    chained()
                    chain(dve.tensor_tensor(rest1[:, :, :], value[:, :, :], part[0][:, :, :], ALU.subtract))
                    chained()
                    if not e.mlp:
                        dve.sem_inc(e.rows_used[s], 1)
                    chain(dve.tensor_copy(part[1][:, :, :], rest1[:, :, :]))
                    chained()
                    chain(dve.tensor_tensor(rest2[:, :, :], rest1[:, :, :], part[1][:, :, :], ALU.subtract))
                    chained()
                    chain(dve.tensor_copy(part[2][:, :, :], rest2[:, :, :]))
                    chained()
                    for k in range(SPLITS):
                        ins = dve.tensor_tensor(spread[s][:, k, :, :, :],
                                                part[k][:, :, :].unsqueeze(2).to_broadcast([P, TILES, H, F]),
                                                hot_h[s][:, :, :].unsqueeze(3).to_broadcast([P, TILES, H, F]), ALU.mult)
                    ins.then_inc(e.spreads[s], 1)
                    assert at["n"] == per

                pairs(dve, step)
                step(GROUPS - 1, PAIRS, 0)
                dve.wait_ge(e.summed, 1)

            def normed(mean_at, sq_name, var_name, sqrt_at, out_col, last):
                dve.wait_ge(p_done, mean_at)
                done(dve.tensor_tensor(ta[:, :], ta[:, :], node_ps[:, 0:L], ALU.subtract))
                after()
                done(dve.tensor_tensor(tc[:, :], ta[:, :], ta[:, :], ALU.mult), sq_name)
                dve.wait_ge(p_done, mean_at + 1)
                done(dve.tensor_scalar(tb[:, :], node_ps[:, 0:L], EPS, None, ALU.add), var_name)
                dve.wait_ge(a_done, sqrt_at)
                done(dve.reciprocal(tb[:, :], tc[:, :]))
                after()
                done(dve.tensor_tensor(out_col, ta[:, :], tb[:, :], ALU.mult), last)
                after()

            edge_pass(conv, rows_xy)
            done(dve.tensor_scalar(rcnt[:, :], cnt[0:H, 0:L], 1.0, None, ALU.max))
            after()
            done(dve.reciprocal(rcnt[:, :], rcnt[:, :]), "rcnt")
            done(dve.tensor_copy(tb[:, :], acc[:, 0:L]))
            dve.wait_ge(p_done, PD["rep"])
            after()
            done(dve.tensor_tensor(tb[:, :], tb[:, :], node_ps[:, 0:L], ALU.mult))
            dve.wait_ge(p_done, PD["root"])
            after()
            done(dve.scalar_tensor_tensor(ta[:, :], hid_ps[:, 0:L], vec["bias"], tb[:, :], ALU.add, ALU.add), "conv_out")
            normed(PD["root"] + 1, "conv_sq", "conv_var", 1, ta[:, :], None)
            done(dve.tensor_scalar(ta[:, :], ta[:, :], vec["ln_w"], vec["ln_b"], ALU.mult, ALU.add))
            after()
            done(dve.tensor_tensor(ta[:, :], ta[:, :], x_col[:, :], ALU.add), "conv_pre")
            dve.wait_ge(a_done, 2)
            done(dve.tensor_tensor(ta[:, :], tb[:, :], x_col[:, :], ALU.add), "res1")
            normed(PD["root"] + 3, "res1_sq", "res1_var", 3, x1_col[:, :], "x1")
            dve.wait_ge(p_done, PD["x1_row"])
            for c, n in CHUNKS:
                done(dve.tensor_copy(x1_row[0:n, c // P, :], node_ps[0:n, c:c + P]), "x1_row" if n < P else None)

            edge_pass(gin1, rows_x)
            done(dve.tensor_scalar(tb[:, :], x1_col[:, :], vec["eps1"], None, ALU.mult))
            after()
            done(dve.tensor_tensor(tb[:, :], tb[:, :], x1_col[:, :], ALU.add))
            after()
            done(dve.tensor_tensor(ta[:, :], tb[:, :], acc[:, 0:L], ALU.add), "gin1_in")
            dve.wait_ge(a_done, A["h1"])
            done(dve.tensor_scalar(h1_col[:, :], h1_col[:, :], 0.0, None, ALU.max), "h1")
            dve.wait_ge(p_done, PD["h1_row"])
            for c, n in CHUNKS:
                done(dve.tensor_copy(h1_row[0:n, c // P, :], node_ps[0:n, c:c + P]), "h1_row" if n < P else None)

            edge_pass(gin2, rows_x)
            done(dve.tensor_scalar(tb[:, :], h1_col[:, :], vec["eps2"], None, ALU.mult))
            after()
            done(dve.tensor_tensor(tb[:, :], tb[:, :], h1_col[:, :], ALU.add))
            after()
            done(dve.tensor_tensor(ta[:, :], tb[:, :], acc[:, 0:L], ALU.add), "gin2_in")
            dve.wait_ge(p_done, PD["logits"])
            for c, n in CHUNKS:
                done(dve.tensor_tensor(y[0:n, 8 * (c // P):8 * (c // P) + 8, :],
                                       hid_ps[0:n, c:c + P].rearrange("p (h f) -> p h f", f=F),
                                       b2b_sb[0:n, :].rearrange("p (h f) -> p h f", f=F), ALU.add))
            after()

            def per_node(col):
                return col[:, :].unsqueeze(2).to_broadcast([P, 4 * H, F])

            done(dve.tensor_reduce(red[:, :], y[:, :, :], AX.X, ALU.max))
            after()
            done(dve.tensor_tensor(y[:, :, :], y[:, :, :], per_node(red), ALU.subtract), "shifted")
            dve.wait_ge(a_done, A["exp"])
            done(dve.tensor_reduce(red[:, :], y2[:, :, :], AX.X, ALU.add), "expsum")
            dve.wait_ge(a_done, A["ln"])
            done(dve.tensor_tensor(y[:, :, :], y[:, :, :], per_node(red2), ALU.subtract))
            after()
            done(dve.tensor_tensor(y[:, :, :], y[:, :, :], x1_row[:, :, :].rearrange("p c (h f) -> p (c h) f", f=F), ALU.add))
            after()
            done(dve.tensor_reduce(red[:, :], y[:, :, :], AX.X, ALU.add))
            after()
            done(dve.tensor_scalar(red[:, :], red[:, :], 1.0 / F, None, ALU.mult))
            after()
            done(dve.tensor_tensor(y[:, :, :], y[:, :, :], per_node(red), ALU.subtract))
            after()
            done(dve.tensor_tensor(y2[:, :, :], y[:, :, :], y[:, :, :], ALU.mult))
            after()
            done(dve.tensor_reduce(red[:, :], y2[:, :, :], AX.X, ALU.add))
            after()
            done(dve.tensor_scalar(red[:, :], red[:, :], 1.0 / F, EPS, ALU.mult, ALU.add), "out_var")
            dve.wait_ge(a_done, A["sqrt"])
            done(dve.reciprocal(red[:, :], red2[:, :]))
            after()
            done(dve.tensor_tensor(y[:, :, :], y[:, :, :], per_node(red), ALU.mult), "out")


V = {"rep": 1, "xy": 9, "rcnt": 11, "conv_out": 14, "conv_sq": 16, "conv_var": 17, "conv_pre": 21, "res1": 22,
     "res1_sq": 24, "res1_var": 25, "x1": 27, "x1_row": 31, "gin1_in": 34, "h1": 35, "h1_row": 39, "gin2_in": 42,
     "shifted": 48, "expsum": 49, "out_var": 57, "out": 59}
A = {"conv_sqrt": 1, "conv_silu": 2, "res1_sqrt": 3, "gin1_mid": 4, "h1": 5, "gin2_mid": 6, "exp": 7, "ln": 8, "sqrt": 9}
PD = {"xB2": 1, "rep": 2, "root": 3, "x1_row": 8, "gin1_a": 9, "gin1_b": 10, "h1_row": 11, "gin2_a": 12, "logits": 13}


def kernel(**inputs):
    import numpy as np
    import concourse.bacc as bacc
    from concourse.bass_utils import run_bass_kernel_spmd

    a = {k: np.asarray(v) for k, v in inputs.items()}
    f32 = np.float32

    x_pad = np.zeros((L * H, F), f32)
    x_pad[:NODES] = a["x"]
    x_rows = x_pad.reshape(L, P)

    slots = GROUPS * TILES * P
    src = np.zeros(slots, np.int32)
    dst = np.full(slots, NODES, np.int32)
    src[:EDGES], dst[:EDGES] = a["src"], a["dst"]
    ids = np.concatenate([v.reshape(GROUPS, TILES, P).transpose(0, 2, 1) for v in (src, dst)], axis=2)

    attr = np.zeros((slots, EDGE_F), f32)
    attr[:EDGES] = a["edge_attr_8"]
    attr = attr.reshape(GROUPS, 2, 2, 2, P, EDGE_F).transpose(0, 2, 5, 1, 3, 4).reshape(GROUPS, 2 * EDGE_F, 4 * P)

    def diagonal(w, n):
        out = np.zeros((n * w.shape[0], n * w.shape[1]), f32)
        for k in range(n):
            out[k * w.shape[0]:(k + 1) * w.shape[0], k * w.shape[1]:(k + 1) * w.shape[1]] = w
        return out

    w1 = diagonal(a["L0_gnn_W1"], 2)
    b1 = np.tile(a["L0_gnn_b1"], 2).reshape(P, 1)
    w2 = a["L0_gnn_W2"].reshape(HIDDEN, F, F).transpose(0, 2, 1).reshape(HIDDEN, F * F)
    w2 = np.concatenate([w2, w2], axis=0)
    mats = {"root": a["L0_gnn_root"], "B2": a["L0_gnn_b2"].reshape(F, F), "w1a": a["L1_gnn_w1a"],
            "w1b": a["L1_gnn_w1b"], "w2a": a["L1_gnn_w2a"], "w2b": a["L1_gnn_w2b"],
            "mean": np.full((F, F), 1.0 / F, f32)}
    vecs = {"bias": a["L0_gnn_bias"], "ln_w": a["L0_gnn_ln_w"], "ln_b": a["L0_gnn_ln_b"], "b1a": a["L1_gnn_b1a"],
            "b1b": a["L1_gnn_b1b"], "b2a": a["L1_gnn_b2a"], "eps1": np.full(F, a["L1_gnn_eps1"]),
            "eps2": np.full(F, a["L1_gnn_eps2"])}
    arrays = {
        "x_rows": x_rows, "x_cols": x_rows.T, "ids": ids, "edge_attr": attr, "w1": w1, "b1": b1, "w2": w2,
        "mats": np.stack([diagonal(mats[n], H) for n in MATS], axis=1),
        "vecs": np.stack([np.tile(vecs[n], H) for n in VECS], axis=1),
        "b2b_row": np.broadcast_to(np.tile(a["L1_gnn_b2b"], H), (P, P)),
        "ident": np.eye(P, dtype=f32),
        "iotas": np.broadcast_to(np.concatenate([np.arange(H), np.arange(LP)]).astype(f32), (P, H + LP)),
    }
    arrays = {k: np.ascontiguousarray(v) for k, v in arrays.items()}
    nc = bacc.Bacc("TRN2", target_bir_lowering=False, num_devices=1)
    args = [nc.dram_tensor(f"in_{k}", v.shape, mybir.dt.from_np(v.dtype), kind="ExternalInput").ap()
            for k, v in arrays.items()]
    out = nc.dram_tensor("out_0", (NODES, F), mybir.dt.float32, kind="ExternalOutput").ap()
    gnn_kernel(nc, *args, out)
    r = run_bass_kernel_spmd(nc, [{f"in_{k}": v for k, v in arrays.items()}], core_ids=[0])
    return r.results[0]["out_0"]
```

```python
import concourse.bass as bass
from concourse import mybir
from contextlib import ExitStack

NODES, F, EDGES = 3125, 16, 103125
EDGE_F, HIDDEN = 8, 64
P = 128
H = P // F
L = -(-NODES // H)
LP = L + L % 2
TILES = 8
UNIT = 2 * TILES
UNITS = -(-EDGES // (P * UNIT))
GROUPS = 2 * UNITS
WINDOW = P // 2
DMA_CONV, DMA_GIN = 12, 6
ONEHOT = UNIT - DMA_GIN
WHOLE = L // P
REST = L - WHOLE * P
BATCH = 3
CHUNKS = [(c, min(P, L - c)) for c in range(0, L, P)]
SPLITS = 3
VECS = ["bias", "ln_w", "ln_b", "b1a", "b1b", "b2a", "eps1", "eps2"]
MATS = ["root", "w1a", "w1b", "w2a", "w2b", "mean"]
EPS = 1e-5
assert UNITS % 2 == 1 and UNITS % BATCH == 0 and SPLITS * REST <= P


def gnn_kernel(nc, x_rows, x_cols, ids, ids_all, src_rows, bases, slot_bases, edge_attr, w1, b1, w2, b2, mats, vecs,
               b2b_row, ident, iota_cols, slot_iota, columns, out):
    f32, bf16, f16, i32 = mybir.dt.float32, mybir.dt.bfloat16, mybir.dt.float16, mybir.dt.int32
    ALU, ACT, AX = mybir.AluOpType, mybir.ActivationFunctionType, mybir.AxisListType

    ctx = ExitStack()
    with ctx:
        def sb(name, shape, dt):
            return ctx.enter_context(nc.sbuf_tensor(name, shape, dt))

        def ps(name, shape, dt=f32):
            return ctx.enter_context(nc.psum_tensor(name, shape, dt))

        def sem(name):
            return ctx.enter_context(nc.semaphore(name))

        table_x1 = nc.dram_tensor("table_x1", (L * H, F), f32, kind="Internal").ap()
        l_rows = nc.dram_tensor("l_rows", (UNITS, UNIT * P), f16, kind="Internal").ap()
        table_h1 = nc.dram_tensor("table_h1", (L * H, F), f32, kind="Internal").ap()

        def scope():
            stack = ctx.enter_context(ExitStack())
            return stack, lambda name, shape, dt: stack.enter_context(nc.sbuf_tensor(name, shape, dt))

        stack, early = scope()
        ids_all_sb = early("ids_all_sb", [P, GROUPS, 2 * TILES], i32)
        src_rows_sb = early("src_rows_sb", [GROUPS, P * TILES], i32)
        src_l_rows = early("src_l_rows", [GROUPS, P * TILES], f16)
        src_h_sb = early("src_h_sb", [P, GROUPS, TILES], i32)
        local_dst = early("local_dst", [P, GROUPS, TILES], f32)
        stack.close()
        slot_l = sb("slot_l", [P, UNITS, LP], bf16)

        stack, early = scope()
        slot_v = early("slot_v", [P, UNITS, F], f32)
        slot_left = early("slot_left", [P, UNITS, F], f32)
        slot_parts = early("slot_parts", [P, UNITS, SPLITS, F], bf16)
        slot_spread = [early(f"slot_spread{j}", [P, SPLITS, H, F], bf16) for j in range(BATCH)]
        slot_cnt = [early(f"slot_cnt{j}", [P, H], f16) for j in range(BATCH)]
        stack.close()
        prod = [sb(f"prod{q}", [P, 4, F, F], f32) for q in range(2)]
        src_hot = [sb(f"src_hot{s}", [P, WHOLE + 1, ONEHOT * P], bf16) for s in range(2)]
        picked = sb("picked", [P, ONEHOT, H, F], f32)

        w1_sb = sb("w1_sb", [2 * EDGE_F, P], f32)
        b1_sb = sb("b1_sb", [P, 1], f32)
        w2_sb = sb("w2_sb", [P, 2 * F * F], f32)
        b2_sb = sb("b2_sb", [SPLITS, 2, F * F], f32)
        b2_left = sb("b2_left", [SPLITS, 2, 2, F * F], f32)
        b2_part = sb("b2_part", [SPLITS, SPLITS - 1, 2, F * F], bf16)
        b2_rows = sb("b2_rows", [P, 2, F * F], bf16)
        ones_sb = sb("ones_sb", [P, P], bf16)
        mats_sb = sb("mats_sb", [P, len(MATS), P], f32)
        vecs_sb = sb("vecs_sb", [P, len(VECS)], f32)
        b2b_sb = sb("b2b_sb", [P, P], f32)
        ident_sb = sb("ident_sb", [P, P], f32)
        iota_l = sb("iota_l", [P, LP], f16)
        slot_iota_sb = sb("slot_iota_sb", [P, WINDOW * UNIT], f16)
        columns_sb = sb("columns_sb", [P, WHOLE + 4], f32)
        col_slot, col_one = columns_sb[:, WHOLE + 1:WHOLE + 2], columns_sb[:, WHOLE + 2:WHOLE + 3]
        iota_h = iota_l[:, 0:H]
        zero_sb = sb("zero_sb", [P, L], bf16)
        mat = {n: mats_sb[:, k, :] for k, n in enumerate(MATS)}
        vec = {n: vecs_sb[:, k:k + 1] for k, n in enumerate(VECS)}

        ids_sb = [sb(f"ids{s}", [P, 2, 2 * TILES], i32) for s in range(2)]
        ea_sb = [sb(f"ea{s}", [2 * EDGE_F, 2, P * TILES // 2], f32) for s in range(2)]
        hid_sb = [sb(f"hid{s}", [P, 2, P * TILES // 2], f32) for s in range(2)]
        rows = [sb(f"rows{s}", [P, UNIT, 2 * F], f32) for s in range(2)]
        rest1 = sb("rest1", [P, UNIT, F], f32)
        rest2 = sb("rest2", [P, UNIT, F], f32)

        dst_h = sb("dst_h", [P, TILES], i32)
        dst_l = sb("dst_l", [P, TILES], i32)
        dst_hf = sb("dst_hf", [P, TILES], f32)
        dst_lf = sb("dst_lf", [P, TILES], f32)
        hot_h = [sb(f"hot_h{s}", [P, TILES, H], bf16) for s in range(2)]
        msg = sb("msg", [P, TILES, F], f32)
        part = [sb(f"part{k}", [P, TILES, F], bf16) for k in range(SPLITS)]
        hot_l = [slot_l[:, TILES * s:TILES * s + TILES, :] for s in range(2)]
        spread = [src_hot[s][:, :, :].rearrange("p a b -> p (a b)")[:, 0:SPLITS * TILES * P].rearrange(
            "p (k t h f) -> p k t h f", k=SPLITS, t=TILES, h=H) for s in range(2)]

        bases_sb = sb("bases_sb", [P, GROUPS], i32)
        slot_bases_sb = sb("slot_bases_sb", [P, UNITS], i32)
        local16 = sb("local16", [P, UNITS, UNIT], f16)
        masks = sb("masks", [P, UNITS, ONEHOT, H], bf16)
        span = sb("span", [P, 4], f32)
        is_local = sb("is_local", [1, 1], i32)
        slot_n = sb("slot_n", [P, UNITS], i32)
        slot_ni = sb("slot_ni", [P, UNITS], i32)
        slot_neg = sb("slot_neg", [P, UNITS], f32)
        slot_h = sb("slot_h", [P, UNITS, H], bf16)
        slot_tmp = sb("slot_tmp", [P, LP], bf16)
        src_l_b = [sb(f"src_l_b{s}", [P, ONEHOT * P], f16) for s in range(2)]
        table = sb("table", [P, WHOLE + 1, SPLITS, P], bf16)
        table_rest = sb("table_rest", [P, P], bf16)
        parts = [sb(f"parts{s}", [P, UNIT, SPLITS * F + 2], bf16) for s in range(2)]
        dst_hot = [sb(f"dst_hot{s}", [P, WINDOW, UNIT], bf16) for s in range(2)]
        sums = sb("sums", [P, UNITS, SPLITS * F + 1], f32)

        x_row = sb("x_row", [P, 4, H, F], f32)
        x_col = sb("x_col", [P, L], f32)
        x1_col = sb("x1_col", [P, L], f32)
        x1_row = sb("x1_row", [P, 4, P], f32)
        h1_col = sb("h1_col", [P, L], f32)
        h1_row = sb("h1_row", [P, 4, P], f32)
        ta = sb("ta", [P, L], f32)
        tb = sb("tb", [P, L], f32)
        tc = sb("tc", [P, L], f32)
        rcnt = sb("rcnt", [H, L], f32)
        rep = sb("rep", [H, P], f32)
        y = sb("y", [P, 4 * H, F], f32)
        y2 = sb("y2", [P, 4 * H, F], f32)
        red = sb("red", [P, 4 * H], f32)
        red2 = sb("red2", [P, 4 * H], f32)

        bank = ps("bank", [P, 8, 512])
        acc, cnt, hid_ps, we_ps, node_ps = bank[:, 0, :], bank[:, 1, :], bank[:, 2, :], bank[:, 3:7, :], bank[:, 7, :]

        def local_ps(e, s):
            return bank[:, 1, P * s:P * s + P] if e.mlp else bank[:, s, 0:P]

        def gather_bank(e, s):
            return 7 * s if e.mlp else 2 + 3 * s

        consts_in = sem("consts_in")
        x_in = sem("x_in")
        ids_all_in = sem("ids_all_in")
        consts_ready = sem("consts_ready")
        table_in = sem("table_in")
        v_done = sem("v_done")
        a_done = sem("a_done")
        p_done = sem("p_done")
        out_done = sem("out_done")
        zeroed = sem("zeroed")
        setup = sem("setup")
        span_sum = sem("span_sum")
        form_known = sem("form_known")
        src_l_ready = sem("src_l_ready")
        l_rows_in = sem("l_rows_in")
        slot_hots = sem("slot_hots")
        sums_done = [sem(f"sums_done{k}") for k in range(3)]

        class Local:
            def __init__(self, name, mlp, by_dma, summed):
                self.mlp, self.by_dma, self.summed = mlp, by_dma, summed
                self.onehot = UNIT - by_dma
                self.ids_in = [sem(f"{name}_ids_in{s}") for s in range(2)]
                self.l_in = [sem(f"{name}_l_in{s}") for s in range(2)]
                self.rows_in = [sem(f"{name}_rows_in{s}") for s in range(2)]
                self.rows_used = sem(f"{name}_rows_used")
                self.turns = sem(f"{name}_turns")
                self.src_hots = [sem(f"{name}_src_hots{s}") for s in range(2)]
                self.gathered = [sem(f"{name}_gathered{s}") for s in range(2)]
                self.picks = [sem(f"{name}_picks{s}") for s in range(2)]
                self.chain = sem(f"{name}_chain")
                self.values = sem(f"{name}_values")
                self.part1 = sem(f"{name}_part1")
                self.rest1 = sem(f"{name}_rest1")
                self.part2 = sem(f"{name}_part2")
                self.rest2 = sem(f"{name}_rest2")
                self.part3 = sem(f"{name}_part3")
                self.dst_hots = sem(f"{name}_dst_hots")
                self.summed_unit = [sem(f"{name}_summed_unit{s}") for s in range(2)]
                self.stored = sem(f"{name}_stored")
                self.table = sem(f"{name}_table")
                self.table_steps = sem(f"{name}_table_steps")
                self.table_rest = sem(f"{name}_table_rest")
                self.slots = sem(f"{name}_slots")
                self.spreads = [sem(f"{name}_slot_spreads{j}") for j in range(BATCH)]
                self.spreads_used = [sem(f"{name}_slot_spreads_used{j}") for j in range(BATCH)]
                if mlp:
                    self.ea_in = [sem(f"{name}_ea_in{s}") for s in range(2)]
                    self.hid_made = sem(f"{name}_hid_made")
                    self.silu = [sem(f"{name}_silu{s}") for s in range(2)]
                    self.we_made = [sem(f"{name}_we_made{b}") for b in range(2)]
                    self.we_read = [sem(f"{name}_we_read{b}") for b in range(2)]
                    self.chain2 = sem(f"{name}_chain2")
                    self.reduced = sem(f"{name}_reduced")

        class Edges:
            def __init__(self, name, local):
                self.mlp, self.summed = local.mlp, local.summed
                self.ids_in, self.rows_in, self.turns, self.hots, self.vec = (
                    local.ids_in, local.rows_in, local.turns, local.src_hots, local.chain)
                self.ids_used, self.spreads = [local.part1, local.part2], [local.rest1, local.rest2]
                self.rows_used, self.scattered = local.picks, local.summed_unit
                if self.mlp:
                    self.ea_in, self.silu, self.hid_made = local.ea_in, local.silu, local.hid_made
                    self.we_read = local.we_read
                    self.hid_read = sem(f"{name}_hid_read")
                    self.we_made = [[sem(f"{name}_we_made{q}{s}") for s in range(2)] for q in range(2)]

        lconv, lgin1, lgin2 = (Local(n, n == "conv", DMA_CONV if n == "conv" else DMA_GIN, d)
                               for n, d in zip(("conv", "gin1", "gin2"), sums_done))
        conv, gin1, gin2 = (Edges(f"general_{n}", l) for n, l in (("conv", lconv), ("gin1", lgin1), ("gin2", lgin2)))

        def pairs(eng, step, first=0, last=GROUPS // 2):
            with eng.Fori(first, last) as i:
                for s in range(2):
                    step(2 * i + s, i, s)

        def next_of(u, i, s):
            return u + 1, (i + 1 if s else i), 1 - s

        def second_of(u, i, s):
            return u + 2, i + 1, s

        def all_units(eng, step):
            for s in range(2):
                step(s, 0, s, 2)
            pairs(eng, lambda u, i, s: step(u, i, s, 2), first=1, last=UNITS // 2 - 1)
            for u in range(UNITS - 3, UNITS):
                step(u, u // 2, u % 2, UNITS - 1 - u)

        def in_form(eng, local, general):
            with eng.If(form[eng.engine]):
                local()
            with eng.Else():
                general()

        form = {}

        def learn_form(eng):
            eng.wait_ge(form_known, 1)
            form[eng.engine] = eng.value_load(is_local[0:1, 0:1], min_val=0, max_val=1)

        block = ctx.enter_context(nc.Block())

        @block.sync
        def _(sp):
            sp.dma_start(src_rows_sb[:, :], src_rows).then_inc(ids_all_in, 16)
            sp.dma_start(ids_all_sb[:, :, :], ids_all).then_inc(ids_all_in, 16)
            sp.dma_start(bases_sb[:, :], bases.to_broadcast([P, GROUPS])).then_inc(ids_all_in, 16)
            for k in range(2):
                sp.dma_start(slot_bases_sb[WINDOW * k:WINDOW * k + WINDOW, :],
                             slot_bases[k:k + 1, :].to_broadcast([WINDOW, UNITS])).then_inc(ids_all_in, 16)
            for dst, src in ((columns_sb, columns), (slot_iota_sb, slot_iota), (iota_l, iota_cols), (w1_sb, w1), (b1_sb, b1),
                             (w2_sb, w2), (vecs_sb, vecs), (b2b_sb, b2b_row), (ident_sb, ident)):
                sp.dma_start(dst[:, :], src).then_inc(consts_in, 16)
            sp.wait_ge(zeroed, 1)
            for c, n in CHUNKS:
                sp.dma_start(x_row[0:n, c // P, :, :], x_rows[c:c + n, :].rearrange("l (h f) -> l h f", f=F)).then_inc(x_in, 16)
            sp.dma_start(x_col[:, :], x_cols).then_inc(x_in, 16)
            sp.dma_start(b2_sb[:, :, :], b2).then_inc(consts_in, 16)
            sp.dma_start(mats_sb[:, :, :], mats).then_inc(x_in, 16)
            sp.wait_ge(src_l_ready, 1)
            sp.dma_start(l_rows.rearrange("u (g n) -> (u g) n", g=2), src_l_rows[:, :]).then_inc(l_rows_in, 16)
            sp.wait_ge(l_rows_in, 16)
            learn_form(sp)

            def write_table(table, rows, width):
                for c, n in CHUNKS:
                    sp.dma_start(table.rearrange("(l h) f -> l (h f)", h=H)[c:c + n, :],
                                 rows[0:n, c // P, :]).then_inc(table_in, 16)

            def feed(e):
                def load(g, i, s, fresh=False):
                    if not fresh:
                        sp.wait_ge(e.rows_in[s], 16 * TILES * i)
                        sp.wait_ge(e.ids_used[s], i)
                    sp.dma_start(ids_sb[s][:, 0, :], ids[bass.ds(g, 1), :, :].rearrange("o p n -> p (o n)")).then_inc(e.ids_in[s], 16)
                    if e.mlp:
                        if not fresh:
                            sp.wait_ge(e.silu[s], i)
                        sp.dma_start(ea_sb[s][:, 0, :], edge_attr[bass.ds(g, 1), :, :].rearrange("o k n -> k (o n)")).then_inc(e.ea_in[s], 16)
                for g in range(2):
                    load(g, 0, g, fresh=True)
                pairs(sp, load, first=1)

            def feed_local(e):
                sp.wait_ge(e.table, 1)
                for k in range(SPLITS):
                    sp.dma_start(table_rest[REST * k:REST * k + REST, :], table[0:REST, WHOLE, k, :]).then_inc(e.table_rest, 16)

                def load(u, i, s, fresh=False):
                    if not fresh:
                        sp.wait_ge(e.src_hots[s], i)
                    sp.dma_start(src_l_b[s][:, 0:e.onehot * P],
                                 l_rows[bass.ds(u, 1), e.by_dma * P:].to_broadcast([P, e.onehot * P])).then_inc(e.l_in[s], 16)
                    if not fresh:
                        sp.wait_ge(e.rows_in[s], 16 * e.by_dma * i)
                    sp.dma_start(ids_sb[s][:, :, :], ids[bass.ds(2 * u, 2), :, :].rearrange("g p n -> p g n")).then_inc(e.ids_in[s], 16)
                    if e.mlp:
                        if not fresh:
                            sp.wait_ge(e.silu[s], 2 * i)
                        sp.dma_start(ea_sb[s][:, :, :], edge_attr[bass.ds(2 * u, 2), :, :].rearrange("g k n -> k g n")).then_inc(e.ea_in[s], 16)
                for s in range(2):
                    load(s, 0, s, fresh=True)
                pairs(sp, load, first=1, last=UNITS // 2)
                load(UNITS - 1, UNITS // 2, 0)

            in_form(sp, lambda: feed_local(lconv), lambda: feed(conv))
            sp.wait_ge(v_done, V["x1_row"])
            write_table(table_x1, x1_row, F)
            in_form(sp, lambda: feed_local(lgin1), lambda: feed(gin1))
            sp.wait_ge(v_done, V["h1_row"])
            write_table(table_h1, h1_row, F)
            in_form(sp, lambda: feed_local(lgin2), lambda: feed(gin2))
            sp.wait_ge(v_done, V["out"])
            y_rows = y[:, :, :].rearrange("p (c h) f -> p c (h f)", h=H)
            o_flat = out.rearrange("n f -> (n f)")
            full = NODES // H
            for c, n in CHUNKS:
                m = min(n, full - c)
                sp.dma_start(o_flat[c * P:(c + m) * P].rearrange("(l k) -> l k", k=P), y_rows[0:m, c // P, :]).then_inc(out_done, 16)
            tail = (NODES - full * H) * F
            c, m = CHUNKS[-1][0], full - CHUNKS[-1][0]
            sp.dma_start(o_flat[full * P:NODES * F].rearrange("(o k) -> o k", o=1), y_rows[m:m + 1, c // P, 0:tail]).then_inc(out_done, 16)
            sp.wait_ge(out_done, 16 * (len(CHUNKS) + 1))

        @block.gpsimd
        def _(pool):
            learn_form(pool)

            def gather(e, table):
                def step(g, i, s):
                    pool.wait_ge(e.ids_in[s], 16 * (i + 1))
                    pool.wait_ge(e.rows_used[s], i + 1)
                    pool.sem_inc(e.turns, 1)
                    for t in range(TILES):
                        pool.indirect_dma_start(
                            out=rows[s][:, t, F:2 * F], out_offset=None, in_=table,
                            in_offset=bass.IndirectOffsetOnAxis(ap=ids_sb[s][:, 0, t:t + 1], axis=0),
                        ).then_inc(e.rows_in[s], 16)
                pairs(pool, step)

            def gather_local(e, table):
                def step(u, i, s, more):
                    pool.wait_ge(e.ids_in[s], 16 * (i + 1))
                    pool.wait_ge(e.rows_used, u + 1)
                    pool.sem_inc(e.turns, 1)
                    for t in range(e.by_dma):
                        pool.indirect_dma_start(
                            out=rows[s][:, t, F:2 * F], out_offset=None, in_=table,
                            in_offset=bass.IndirectOffsetOnAxis(ap=ids_sb[s][:, t // TILES, t % TILES:t % TILES + 1], axis=0),
                        ).then_inc(e.rows_in[s], 16)
                all_units(pool, step)

            table_x = x_rows.rearrange("l (h f) -> (l h) f", f=F)
            for n, (local, general, tab) in enumerate(((lconv, conv, table_x), (lgin1, gin1, table_x1), (lgin2, gin2, table_h1))):
                if n:
                    pool.wait_ge(table_in, 16 * len(CHUNKS) * n)
                in_form(pool, lambda: gather_local(local, tab), lambda: gather(general, tab))

        @block.tensor
        def _(pe):
            for e in (lconv, lgin1, lgin2):
                for s in range(2):
                    pe.sem_inc(e.gathered[s], 1)
                    pe.sem_inc(e.summed_unit[s], 1)
                for j in range(BATCH):
                    pe.sem_inc(e.spreads_used[j], 1)
            pe.sem_inc(lconv.we_made[1], 3)
            for q in range(2):
                for s in range(2):
                    pe.sem_inc(conv.we_made[q][s], 1)
            def scatter(e, i, s):
                pe.wait_ge(e.hots[s], i + 1)
                pe.wait_ge(e.spreads[s], i + 1)
                for t in range(TILES):
                    for k in range(SPLITS):
                        mm = pe.matmul(acc[:, 0:L], spread[s][:, k, t, :, :].rearrange("p h f -> p (h f)"),
                                       hot_l[s][:, t, 0:L], start=False, stop=False, skip_group_check=True)
                    if e.mlp:
                        mm = pe.matmul(cnt[0:H, 0:L], hot_h[s][:, t, :], hot_l[s][:, t, 0:L],
                                       start=False, stop=False, skip_group_check=True)
                mm.then_inc(e.scattered[s], 1)

            def open_sums(e):
                pe.matmul(acc[:, 0:L], zero_sb[:, 0:P], zero_sb[:, :], start=True, stop=False, skip_group_check=True)
                if e.mlp:
                    pe.matmul(cnt[0:H, 0:L], zero_sb[:, 0:H], zero_sb[:, :], start=True, stop=False, skip_group_check=True)

            def close_sums(e):
                mm = pe.matmul(acc[:, 0:L], zero_sb[:, 0:P], zero_sb[:, :], start=False, stop=True, skip_group_check=True)
                if e.mlp:
                    mm = pe.matmul(cnt[0:H, 0:L], zero_sb[:, 0:H], zero_sb[:, :], start=False, stop=True, skip_group_check=True)
                mm.then_inc(e.summed, 1)

            def weights_of(hid, q):
                for k in range(2):
                    pe.matmul(we_ps[:, 2 * q + k, :], ones_sb[:, :], b2_rows[:, :, :].rearrange("p k n -> p (k n)"),
                              start=True, stop=False, skip_group_check=True)
                    mm = pe.matmul(we_ps[:, 2 * q + k, :], hid[:, P * (2 * q + k):P * (2 * q + k) + P], w2_sb[:, :],
                                   start=False, stop=True, skip_group_check=True)
                return mm

            def hidden(g, i, s):
                pe.wait_ge(conv.ea_in[s], 16 * (i + 1))
                pe.wait_ge(conv.hid_read, g + 1)
                pe.matmul(hid_ps, w1_sb[:, :], ea_sb[s][:, 0, :], start=True, stop=True).then_inc(conv.hid_made, 1)

            def edge_weights(g, i, s):
                pe.wait_ge(conv.silu[s], i + 1)
                for q in range(2):
                    pe.wait_ge(conv.we_read[q], g + 1)
                    weights_of(hid_sb[s][:, 0, :], q).then_inc(conv.we_made[q][s], 1)

            pe.wait_ge(x_in, 16 * (len(CHUNKS) + 2))
            pe.wait_ge(setup, SETUP_SPAN)
            pe.matmul(node_ps[0:1, 0:1], span[:, 2:3], col_one, start=True, stop=True).then_inc(span_sum, 1)
            pe.wait_ge(consts_ready, 1)
            learn_form(pe)

            def gather_onehot(e, u, i, s):
                pe.wait_ge(e.src_hots[s], i + 1)
                pe.wait_ge(e.picks[s], i + 1)
                first = gather_bank(e, s)
                for t in range(e.onehot):
                    dst = bank[:, first + t // 4, P * (t % 4):P * (t % 4) + P]
                    for c in range(WHOLE):
                        for k in range(SPLITS):
                            pe.matmul(dst, src_hot[s][:, c, P * t:P * t + P], table[:, c, k, :],
                                      start=(c == 0 and k == 0), stop=False, skip_group_check=True)
                    mm = pe.matmul(dst, src_hot[s][:, WHOLE, P * t:P * t + P], table_rest[:, :],
                                   start=False, stop=True, skip_group_check=True)
                mm.then_inc(e.gathered[s], 1)

            def sum_unit(e, u, i, s):
                pe.wait_ge(e.part3, u + 2)
                pe.wait_ge(e.dst_hots, u + 1)
                pe.wait_ge(e.stored, u + (2 if e.mlp else 1))
                n = SPLITS * F + (1 if e.mlp else 0)
                for g in range(2):
                    for t in range(TILES):
                        mm = pe.matmul(local_ps(e, s)[WINDOW * g:WINDOW * g + WINDOW, 0:n], dst_hot[s][:, :, TILES * g + t],
                                       parts[s][:, TILES * g + t, 0:n], start=(t == 0), stop=(t == TILES - 1))
                mm.then_inc(e.summed_unit[s], 1)

            def hidden_local(u, i, s, k):
                if k == 0:
                    pe.wait_ge(lconv.ea_in[s], 16 * (i + 1))
                    if not (isinstance(u, int) and u == 0):
                        pe.wait_ge(lconv.silu[1 - s], 2 * (i + s))
                else:
                    pe.wait_ge(lconv.silu[s], 2 * i + 1)
                pe.matmul(hid_ps, w1_sb[:, :], ea_sb[s][:, k, :], start=True, stop=True).then_inc(lconv.hid_made, 1)

            def edge_weights_local(u, i, s, quads):
                pe.wait_ge(lconv.silu[s], 2 * (i + 1))
                for q in quads:
                    pe.wait_ge(lconv.we_read[q % 2], 2 * u + q // 2 + 1)
                    weights_of(hid_sb[s][:, q // 2, :], q % 2).then_inc(lconv.we_made[q % 2], 1)

            def local_pass(e):
                pe.wait_ge(e.table_rest, 16 * SPLITS)
                for s in range(2):
                    gather_onehot(e, s, 0, s)
                    if e.mlp:
                        for k in range(2):
                            hidden_local(s, 0, s, k)
                if e.mlp:
                    edge_weights_local(0, 0, 0, (0, 1))

                def step(u, i, s, more):
                    if e.mlp:
                        edge_weights_local(u, i, s, (2, 3))
                        if more:
                            edge_weights_local(*next_of(u, i, s), (0, 1))
                        if more == 2:
                            hidden_local(*second_of(u, i, s), 0)
                    if not (isinstance(u, int) and u == 0):
                        sum_unit(e, u - 1, (i if s else i - 1), 1 - s)
                    if more == 2:
                        gather_onehot(e, *second_of(u, i, s))
                        if e.mlp:
                            hidden_local(*second_of(u, i, s), 1)
                all_units(pe, step)
                sum_unit(e, UNITS - 1, UNITS // 2, 0)
                pe.wait_ge(e.stored, UNITS + 2)
                open_sums(e)
                with pe.Fori(0, UNITS // BATCH) as i:
                    for j in range(BATCH):
                        pe.wait_ge(e.spreads[j], i + 1)
                        cols_l = slot_l[:, bass.ds(BATCH * i + j, 1), 0:L].rearrange("p o l -> p (o l)")
                        if e.mlp:
                            pe.matmul(cnt[0:H, 0:L], slot_cnt[j][:, :], cols_l, start=False, stop=False, skip_group_check=True)
                        for k in range(SPLITS):
                            mm = pe.matmul(acc[:, 0:L], slot_spread[j][:, k, :, :].rearrange("p h f -> p (h f)"), cols_l,
                                           start=False, stop=False, skip_group_check=True)
                        mm.then_inc(e.spreads_used[j], 1)
                close_sums(e)

            def conv_step(g, i, s):
                hidden(g, i, s)
                scatter(conv, i - 1, s)
                edge_weights(g, i, s)

            def general_conv():
                open_sums(conv)
                for g in range(2):
                    hidden(g, 0, g)
                    edge_weights(g, 0, g)
                pairs(pe, conv_step, first=1)
                for s in range(2):
                    scatter(conv, GROUPS // 2 - 1, s)
                close_sums(conv)

            in_form(pe, lambda: local_pass(lconv), general_conv)

            def cols(dst, weights, src, v):
                pe.wait_ge(v_done, v)
                pe.matmul(dst, weights, src, start=True, stop=True).then_inc(p_done, 1)

            def acols(dst, weights, src, a):
                pe.wait_ge(a_done, a)
                pe.matmul(dst, weights, src, start=True, stop=True).then_inc(p_done, 1)

            def to_rows(dst, src, v):
                pe.wait_ge(v_done, v)
                for c, n in CHUNKS:
                    mm = pe.transpose(dst[0:n, c:c + P], src[:, c:c + n], ident_sb[:, :])
                mm.then_inc(p_done, 1)

            node, big = node_ps[:, 0:L], bank[:, 2, 0:L]
            cols(node, rep[:, :], rcnt[:, :], V["rcnt"])
            pe.matmul(big, mat["root"], x_col[:, :], start=True, stop=True).then_inc(p_done, 1)
            cols(node, mat["mean"], ta[:, :], V["conv_out"])
            cols(node, mat["mean"], tc[:, :], V["conv_sq"])
            cols(node, mat["mean"], ta[:, :], V["res1"])
            cols(node, mat["mean"], tc[:, :], V["res1_sq"])
            to_rows(node_ps, x1_col, V["x1"])

            def gin(e):
                open_sums(e)
                pairs(pe, lambda g, i, s: scatter(e, i, s))
                close_sums(e)

            in_form(pe, lambda: local_pass(lgin1), lambda: gin(gin1))
            cols(node, mat["w1a"], ta[:, :], V["gin1_in"])
            acols(big, mat["w1b"], tb[:, :], A["gin1_mid"])
            to_rows(node_ps, h1_col, V["h1"])
            in_form(pe, lambda: local_pass(lgin2), lambda: gin(gin2))
            cols(node, mat["w2a"], ta[:, :], V["gin2_in"])
            pe.wait_ge(a_done, A["gin2_mid"])
            for c, n in CHUNKS:
                mm = pe.matmul(hid_ps[0:n, c:c + P], tb[:, c:c + n], mat["w2b"], start=True, stop=True)
            mm.then_inc(p_done, 1)

        @block.scalar
        def _(act):
            act.sem_inc(conv.hid_read, 1)
            for e in (lconv, lgin1, lgin2):
                act.sem_inc(e.part3, 1)
                act.sem_inc(e.stored, 2)
            act.wait_ge(consts_ready, 1)
            learn_form(act)

            def silu_local(u, i, s, k):
                act.wait_ge(lconv.hid_made, 2 * u + k + 1)
                act.wait_ge(lconv.we_made[1], 2 * u + 1)
                act.activation(hid_sb[s][:, k, :], hid_ps, ACT.Silu, bias=b1_sb[:, 0:1]).then_inc(lconv.silu[s], 1)

            def store(e, u, i, s):
                act.wait_ge(e.summed_unit[s], i + 2)
                n = SPLITS * F + (1 if e.mlp else 0)
                act.activation(sums[:, bass.ds(u, 1), 0:n].rearrange("p o n -> p (o n)"), local_ps(e, s)[:, 0:n], ACT.Copy).then_inc(e.stored, 1)

            def local_pass(e):
                def step(u, i, s, more):
                    value = rows[s][:, :, 0:F] if e.mlp else rows[s][:, :, F:2 * F]
                    act.wait_ge(e.rows_in[s], 16 * e.by_dma * (i + 1))
                    act.wait_ge(e.values, u + 1)
                    act.wait_ge(e.summed_unit[s], i + 1)
                    act.activation(parts[s][:, :, 0:F], value, ACT.Copy).then_inc(e.part1, 1)
                    if e.mlp:
                        if not (isinstance(u, int) and u == 0):
                            act.wait_ge(slot_hots, 2 * u)
                        act.activation(slot_tmp[:, :], iota_l[:, :], ACT.Abs, bias=slot_neg[:, bass.ds(u, 1)]).then_inc(slot_hots, 1)
                    act.wait_ge(e.rest1, u + 1)
                    act.activation(parts[s][:, :, F:2 * F], rest1[:, :, :], ACT.Copy).then_inc(e.part2, 1)
                    if e.mlp:
                        act.wait_ge(slot_hots, 2 * u + 1)
                        act.activation(slot_l[:, bass.ds(u, 1), :].rearrange("p o l -> p (o l)"), slot_tmp[:, :], ACT.Relu,
                                       scale=-1.0, bias=col_one).then_inc(slot_hots, 1)
                    act.wait_ge(e.rest2, u + 1)
                    act.activation(parts[s][:, :, 2 * F:3 * F], rest2[:, :, :], ACT.Copy).then_inc(e.part3, 1)
                    if e.mlp and more == 2:
                        silu_local(*second_of(u, i, s), 0)
                    if not (isinstance(u, int) and u == 0):
                        store(e, u - 1, (i if s else i - 1), 1 - s)
                    if e.mlp and more == 2:
                        silu_local(*second_of(u, i, s), 1)
                if e.mlp:
                    for s in range(2):
                        for k in range(2):
                            silu_local(s, 0, s, k)
                all_units(act, step)
                store(e, UNITS - 1, UNITS // 2, 0)

            def silu(g, i, s):
                act.wait_ge(conv.hid_made, g + 1)
                act.wait_ge(conv.we_made[1][s], i + 1)
                act.activation(hid_sb[s][:, 0, :], hid_ps, ACT.Silu, bias=b1_sb[:, 0:1]).then_inc(conv.silu[s], 1)
                act.wait_ge(conv.silu[s], i + 1)
                act.sem_inc(conv.hid_read, 1)
            in_form(act, lambda: local_pass(lconv), lambda: pairs(act, silu))

            def one(v, dst, src, fn, **kw):
                act.wait_ge(v_done, v)
                act.activation(dst, src, fn, **kw).then_inc(a_done, 1)
            one(V["conv_var"], tc[:, :], tb[:, :], ACT.Sqrt)
            one(V["conv_pre"], tb[:, :], ta[:, :], ACT.Silu)
            one(V["res1_var"], tc[:, :], tb[:, :], ACT.Sqrt)
            in_form(act, lambda: local_pass(lgin1), lambda: act.nop())
            act.wait_ge(p_done, PD["gin1_a"])
            act.activation(tb[:, :], node_ps[:, 0:L], ACT.Relu, bias=vec["b1a"]).then_inc(a_done, 1)
            act.wait_ge(p_done, PD["gin1_b"])
            act.activation(h1_col[:, :], hid_ps[:, 0:L], ACT.Relu, bias=vec["b1b"]).then_inc(a_done, 1)
            in_form(act, lambda: local_pass(lgin2), lambda: act.nop())
            act.wait_ge(p_done, PD["gin2_a"])
            act.activation(tb[:, :], node_ps[:, 0:L], ACT.Relu, bias=vec["b2a"]).then_inc(a_done, 1)
            one(V["shifted"], y2[:, :, :], y[:, :, :], ACT.Exp)
            one(V["expsum"], red2[:, :], red[:, :], ACT.Ln)
            one(V["out_var"], red2[:, :], red[:, :], ACT.Sqrt)

        @block.vector
        def _(dve):
            state = {"v": 0}

            def done(ins, name=None):
                state["v"] += 1
                ins.then_inc(v_done, 1)
                if name:
                    assert V[name] == state["v"], (name, state["v"])

            def after():
                dve.wait_ge(v_done, state["v"])

            for e in (lconv, lgin1, lgin2):
                dve.sem_inc(e.rows_used, 2)
                for s in range(2):
                    dve.sem_inc(e.picks[s], 1)
            for q in range(2):
                dve.sem_inc(lconv.we_read[q], 1)

            steps = {"n": 0}

            def chain(ins):
                steps["n"] += 1
                ins.then_inc(setup, 1)

            def chained():
                dve.wait_ge(setup, steps["n"])

            dve.memset(x_row[:, WHOLE, :, :], 0.0).then_inc(zeroed, 1)
            dve.memset(zero_sb[:, :], 0.0)
            dve.memset(ones_sb[:, :], 1.0)
            dve.memset(b2_rows[:, :, :], 0.0)
            dve.memset(table_rest[:, :], 0.0)
            dve.memset(x1_row[:, 3, :], 0.0)
            dve.memset(h1_row[:, 3, :], 0.0)
            dve.memset(parts[0][:, :, :], 1.0)
            dve.memset(parts[1][:, :, :], 1.0)
            chain(dve.memset(y[:, :, :], 0.0))
            dve.wait_ge(ids_all_in, 16 * 5)
            chain(dve.tensor_scalar(src_rows_sb[:, :], src_rows_sb[:, :], 3, None, ALU.logical_shift_right))
            chained()
            dve.tensor_copy(src_l_rows[:, :], src_rows_sb[:, :]).then_inc(src_l_ready, 1)
            chain(dve.tensor_tensor(local_dst[:, :, :], ids_all_sb[:, :, TILES:],
                                    bases_sb[:, :].unsqueeze(2).to_broadcast([P, GROUPS, TILES]), ALU.subtract))
            chain(dve.tensor_scalar(src_h_sb[:, :, :], ids_all_sb[:, :, 0:TILES], H - 1, None, ALU.bitwise_and))
            dve.wait_ge(consts_in, 16 * 10)
            chain(dve.tensor_scalar(slot_n[:, :], slot_bases_sb[:, :], col_slot, None, ALU.add))
            chained()
            dve.tensor_reduce(span[:, 0:1], local_dst[:, :, :], AX.XY, ALU.max)
            chain(dve.tensor_reduce(span[:, 1:2], local_dst[:, :, :], AX.XY, ALU.min))
            chained()
            dve.tensor_scalar(span[:, 0:1], span[:, 0:1], float(WINDOW), None, ALU.is_ge)
            chain(dve.tensor_scalar(span[:, 1:2], span[:, 1:2], 0.0, None, ALU.is_lt))
            chained()
            chain(dve.tensor_tensor(span[:, 2:3], span[:, 0:1], span[:, 1:2], ALU.add))
            assert SETUP_SPAN == steps["n"]
            dve.tensor_copy(local16[:, :, :].rearrange("p u t -> p (u t)"), local_dst[:, :, :].rearrange("p g t -> p (g t)"))
            dve.tensor_scalar(slot_ni[:, :], slot_n[:, :], 3, None, ALU.logical_shift_right)
            chain(dve.tensor_scalar(slot_n[:, :], slot_n[:, :], H - 1, None, ALU.bitwise_and))
            chained()
            dve.tensor_tensor(masks[:, :, :, :],
                              src_h_sb[:, :, :].rearrange("p g t -> p (g t)").rearrange("p (u t) -> p u t", t=UNIT)[:, :, DMA_GIN:]
                              .unsqueeze(3).to_broadcast([P, UNITS, ONEHOT, H]),
                              iota_h.unsqueeze(1).unsqueeze(1).to_broadcast([P, UNITS, ONEHOT, H]), ALU.is_equal)
            dve.tensor_tensor(slot_h[:, :, :], slot_n[:, :].unsqueeze(2).to_broadcast([P, UNITS, H]),
                              iota_h.unsqueeze(1).to_broadcast([P, UNITS, H]), ALU.is_equal)
            dve.tensor_scalar(slot_neg[:, :], slot_ni[:, :], -1.0, None, ALU.mult)
            chain(dve.tensor_copy(b2_part[:, 0, :, :], b2_sb[:, :, :]))
            chained()
            chain(dve.tensor_tensor(b2_left[:, 0, :, :], b2_sb[:, :, :], b2_part[:, 0, :, :], ALU.subtract))
            chained()
            chain(dve.tensor_copy(b2_part[:, 1, :, :], b2_left[:, 0, :, :]))
            chained()
            chain(dve.tensor_tensor(b2_left[:, 1, :, :], b2_left[:, 0, :, :], b2_part[:, 1, :, :], ALU.subtract))
            chained()
            keep = [ident_sb[0:SPLITS, k:k + 1] for k in range(SPLITS)]
            chain(dve.tensor_scalar(b2_left[:, 1, :, :], b2_left[:, 1, :, :], keep[2], None, ALU.mult))
            for k in range(2):
                chained()
                ins = dve.scalar_tensor_tensor(b2_rows[0:SPLITS, :, :] if k else b2_left[:, 1, :, :], b2_part[:, k, :, :], keep[k],
                                               b2_left[:, 1, :, :], ALU.mult, ALU.add)
                if k == 0:
                    chain(ins)
            ins.then_inc(consts_ready, 1)
            dve.wait_ge(span_sum, 1)
            dve.tensor_scalar(is_local[:, :], node_ps[0:1, 0:1], 0.0, None, ALU.is_equal).then_inc(form_known, 1)
            dve.wait_ge(x_in, 16 * (len(CHUNKS) + 2))
            done(dve.tensor_copy(rep[:, :].rearrange("k (h f) -> k h f", f=F),
                                 ident_sb[0:H, 0:H].unsqueeze(2).to_broadcast([H, H, F])), "rep")
            learn_form(dve)
            dve.wait_ge(consts_ready, 1)

            def build_table(e, source):
                whole = source.rearrange("p c n -> p (c n)").rearrange("p (c n) -> p c n", n=P)
                left = picked[:, 0:4, :, :].rearrange("p c h f -> p c (h f)")
                at = {"n": 0}

                def part_chain(ins):
                    at["n"] += 1
                    ins.then_inc(e.table_steps, 1)
                    dve.wait_ge(e.table_steps, at["n"])
                part_chain(dve.tensor_copy(table[:, :, 0, :], whole))
                part_chain(dve.tensor_tensor(left, whole, table[:, :, 0, :], ALU.subtract))
                part_chain(dve.tensor_copy(table[:, :, 1, :], left))
                part_chain(dve.tensor_tensor(left, left, table[:, :, 1, :], ALU.subtract))
                dve.tensor_copy(table[:, :, 2, :], left).then_inc(e.table, 1)

            def source_hots(e, u, i, s, chunks):
                n = e.onehot * P
                for c in chunks:
                    if c == 0:
                        dve.wait_ge(e.l_in[s], 16 * (i + 1))
                        dve.wait_ge(e.gathered[s], i + 1)
                    ins = dve.tensor_scalar(src_hot[s][:, c, 0:n], src_l_b[s][:, 0:n], columns_sb[:, c:c + 1], None, ALU.is_equal)
                    if c == WHOLE:
                        ins.then_inc(e.src_hots[s], 1)

            def dest_hots(e, u, i, s):
                dve.wait_ge(e.summed_unit[s], i + 1)
                dve.tensor_tensor(dst_hot[s][:, :, :], slot_iota_sb[:, :].rearrange("p (w t) -> p w t", t=UNIT),
                                  local16[:, bass.ds(u, 1), :].to_broadcast([P, WINDOW, UNIT]), ALU.is_equal).then_inc(e.dst_hots, 1)

            def local_pass(e, source):
                build_table(e, source)
                for s in range(2):
                    source_hots(e, s, 0, s, range(WHOLE + 1))

                def step(u, i, s, more):
                    dve.wait_ge(e.gathered[s], i + 2)
                    first = gather_bank(e, s)
                    cols_g = bank[:, first:first + -(-e.onehot // 4), :].rearrange("p b n -> p (b n)")[:, 0:e.onehot * P].rearrange(
                        "p (t h f) -> p t h f", h=H, f=F)
                    mid = e.onehot // 2
                    for k, (a, b) in enumerate(((0, mid), (mid, e.onehot))):
                        mask = masks[:, bass.ds(u, 1), ONEHOT - e.onehot + a:ONEHOT - e.onehot + b, :].rearrange(
                            "p o t h -> p (o t) h").unsqueeze(3).to_broadcast([P, b - a, H, F])
                        ins = dve.tensor_tensor(picked[:, a:b, :, :], cols_g[:, a:b, :, :], mask, ALU.mult)
                        ins.then_inc(e.chain if k == 0 else e.picks[s], 1)
                    for k, (a, b) in enumerate(((0, mid), (mid, e.onehot))):
                        if k == 0:
                            dve.wait_ge(e.chain, u + 1)
                        else:
                            dve.wait_ge(e.picks[s], i + 2)
                        ins = dve.tensor_reduce(rows[s][:, e.by_dma + a:e.by_dma + b, F:2 * F],
                                                picked[:, a:b, :, :].rearrange("p t h f -> p t f h"), AX.X, ALU.add)
                    if not e.mlp:
                        ins.then_inc(e.values, 1)
                        dest_hots(e, u, i, s)
                    else:
                        ins.then_inc(e.chain2, 1)
                        dve.wait_ge(e.chain2, u + 1)
                        dve.wait_ge(e.rows_in[s], 16 * e.by_dma * (i + 1))

                        def product(q):
                            dve.wait_ge(e.we_made[q % 2], 2 * u + q // 2 + 1 + 3 * (q % 2))
                            if q >= 2:
                                dve.wait_ge(e.reduced, 3 * u + q - 1)
                            weights = bank[:, 3 + 2 * (q % 2):5 + 2 * (q % 2), :].rearrange("p b (k o i) -> p (b k) o i", k=2, o=F)
                            x_in_edge = rows[s][:, 4 * q:4 * q + 4, F:2 * F].unsqueeze(2).to_broadcast([P, 4, F, F])
                            dve.tensor_tensor(prod[q % 2][:, :, :, :], weights, x_in_edge, ALU.mult).then_inc(e.we_read[q % 2], 1)

                        def reduction(q):
                            dve.wait_ge(e.we_read[q % 2], 2 * u + q // 2 + 2)
                            ins = dve.tensor_reduce(rows[s][:, 4 * q:4 * q + 4, 0:F], prod[q % 2][:, :, :, :], AX.X, ALU.add)
                            ins.then_inc(e.reduced if q < 3 else e.values, 1)
                        product(0)
                        product(1)
                        reduction(0)
                        dest_hots(e, u, i, s)
                        product(2)
                        reduction(1)
                        product(3)
                        reduction(2)
                        reduction(3)
                    value = rows[s][:, :, 0:F] if e.mlp else rows[s][:, :, F:2 * F]
                    if more == 2:
                        source_hots(e, *second_of(u, i, s), (0, 1))
                    dve.wait_ge(e.part1, u + 1)
                    dve.tensor_tensor(rest1[:, :, :], value, parts[s][:, :, 0:F], ALU.subtract).then_inc(e.rest1, 1)
                    if more == 2:
                        source_hots(e, *second_of(u, i, s), (2, 3))
                    dve.wait_ge(e.part2, u + 1)
                    dve.wait_ge(e.rest1, u + 1)
                    dve.sem_inc(e.rows_used, 1)
                    dve.wait_ge(e.part3, u + 1)
                    dve.tensor_tensor(rest2[:, :, :], rest1[:, :, :], parts[s][:, :, F:2 * F], ALU.subtract).then_inc(e.rest2, 1)
                all_units(dve, step)

                dve.wait_ge(e.stored, UNITS + 2)
                at = {"n": 0}

                def chain(ins):
                    at["n"] += 1
                    ins.then_inc(e.slots, 1)
                    dve.wait_ge(e.slots, at["n"])
                chain(dve.tensor_tensor(slot_v[:, :, :], sums[:, :, 0:F], sums[:, :, F:2 * F], ALU.add))
                chain(dve.tensor_tensor(slot_v[:, :, :], slot_v[:, :, :], sums[:, :, 2 * F:3 * F], ALU.add))
                chain(dve.tensor_copy(slot_parts[:, :, 0, :], slot_v[:, :, :]))
                chain(dve.tensor_tensor(slot_left[:, :, :], slot_v[:, :, :], slot_parts[:, :, 0, :], ALU.subtract))
                chain(dve.tensor_copy(slot_parts[:, :, 1, :], slot_left[:, :, :]))
                chain(dve.tensor_tensor(slot_left[:, :, :], slot_left[:, :, :], slot_parts[:, :, 1, :], ALU.subtract))
                chain(dve.tensor_copy(slot_parts[:, :, 2, :], slot_left[:, :, :]))
                with dve.Fori(0, UNITS // BATCH) as i:
                    for j in range(BATCH):
                        unit = bass.ds(BATCH * i + j, 1)
                        dve.wait_ge(e.spreads_used[j], i + 1)
                        if e.mlp:
                            dve.tensor_scalar(slot_cnt[j][:, :], slot_h[:, unit, :].rearrange("p o h -> p (o h)"),
                                              sums[:, unit, SPLITS * F:SPLITS * F + 1].rearrange("p o n -> p (o n)"), None, ALU.mult)
                        dve.tensor_tensor(slot_spread[j][:, :, :, :],
                                          slot_parts[:, unit, :, :].rearrange("p o k f -> p (o k) f").unsqueeze(2).to_broadcast([P, SPLITS, H, F]),
                                          slot_h[:, unit, :].unsqueeze(3).to_broadcast([P, SPLITS, H, F]), ALU.mult).then_inc(e.spreads[j], 1)
                dve.wait_ge(e.summed, 1)

            def edge_pass(e):
                per = 9 if e.mlp else 7
                left1, left2 = rest1[:, 0:TILES, :], rest2[:, 0:TILES, :]

                def step(g, i, s):
                    at = {"n": 0}

                    def chain(ins):
                        at["n"] += 1
                        ins.then_inc(e.vec, 1)

                    def chained(back=0):
                        dve.wait_ge(e.vec, per * g + at["n"] - back)

                    dve.wait_ge(e.ids_in[s], 16 * (i + 1))
                    dve.wait_ge(e.scattered[s], i + 1)
                    dve.tensor_scalar(dst_h[:, :], ids_sb[s][:, 0, TILES:], H - 1, None, ALU.bitwise_and)
                    chain(dve.tensor_scalar(dst_l[:, :], ids_sb[s][:, 0, TILES:], 3, None, ALU.logical_shift_right))
                    chained()
                    dve.tensor_copy(dst_hf[:, :], dst_h[:, :])
                    chain(dve.tensor_copy(dst_lf[:, :], dst_l[:, :]))
                    chained()
                    dve.tensor_tensor(hot_h[s][:, :, :], dst_hf[:, :].unsqueeze(2).to_broadcast([P, TILES, H]),
                                      iota_h.unsqueeze(1).to_broadcast([P, TILES, H]), ALU.is_equal).then_inc(e.ids_used[s], 1)
                    for t in range(TILES):
                        ins = dve.tensor_scalar(hot_l[s][:, t, :], iota_l[:, :], dst_lf[:, t:t + 1], None, ALU.is_equal)
                    ins.then_inc(e.hots[s], 1)
                    dve.wait_ge(e.rows_in[s], 16 * TILES * (i + 1))
                    if e.mlp:
                        for q in range(2):
                            dve.wait_ge(e.we_made[q][s], i + 2)
                            weights = we_ps[:, 2 * q:2 * q + 2, :].rearrange("p b (k o i) -> p (b k) o i", k=2, o=F)
                            x_in_edge = rows[s][:, 4 * q:4 * q + 4, F:2 * F].unsqueeze(2).to_broadcast([P, 4, F, F])
                            dve.tensor_tensor(prod[q][:, :, :, :], weights, x_in_edge, ALU.mult).then_inc(e.we_read[q], 1)
                            dve.wait_ge(e.we_read[q], g + 2)
                            chain(dve.tensor_reduce(msg[:, 4 * q:4 * q + 4, :], prod[q][:, :, :, :], AX.X, ALU.add))
                        chained()
                        dve.sem_inc(e.rows_used[s], 1)
                        value = msg[:, :, :]
                    else:
                        value = rows[s][:, 0:TILES, F:2 * F]
                    chain(dve.tensor_copy(part[0][:, :, :], value))
                    chained()
                    chain(dve.tensor_tensor(left1, value, part[0][:, :, :], ALU.subtract))
                    chained()
                    if not e.mlp:
                        dve.sem_inc(e.rows_used[s], 1)
                    chain(dve.tensor_copy(part[1][:, :, :], left1))
                    chained()
                    chain(dve.tensor_tensor(left2, left1, part[1][:, :, :], ALU.subtract))
                    chained()
                    chain(dve.tensor_copy(part[2][:, :, :], left2))
                    chained()
                    for k in range(SPLITS):
                        ins = dve.tensor_tensor(spread[s][:, k, :, :, :],
                                                part[k][:, :, :].unsqueeze(2).to_broadcast([P, TILES, H, F]),
                                                hot_h[s][:, :, :].unsqueeze(3).to_broadcast([P, TILES, H, F]), ALU.mult)
                    ins.then_inc(e.spreads[s], 1)
                    assert at["n"] == per

                pairs(dve, step)
                dve.wait_ge(e.summed, 1)

            def normed(mean_at, sq_name, var_name, sqrt_at, out_col, last):
                dve.wait_ge(p_done, mean_at)
                done(dve.tensor_tensor(ta[:, :], ta[:, :], node_ps[:, 0:L], ALU.subtract))
                after()
                done(dve.tensor_tensor(tc[:, :], ta[:, :], ta[:, :], ALU.mult), sq_name)
                dve.wait_ge(p_done, mean_at + 1)
                done(dve.tensor_scalar(tb[:, :], node_ps[:, 0:L], EPS, None, ALU.add), var_name)
                dve.wait_ge(a_done, sqrt_at)
                done(dve.reciprocal(tb[:, :], tc[:, :]))
                after()
                done(dve.tensor_tensor(out_col, ta[:, :], tb[:, :], ALU.mult), last)
                after()

            in_form(dve, lambda: local_pass(lconv, x_row[:, :, :, :].rearrange("p c h f -> p c (h f)")), lambda: edge_pass(conv))
            done(dve.tensor_scalar(rcnt[:, :], cnt[0:H, 0:L], 1.0, None, ALU.max))
            after()
            done(dve.reciprocal(rcnt[:, :], rcnt[:, :]), "rcnt")
            done(dve.tensor_copy(tb[:, :], acc[:, 0:L]))
            dve.wait_ge(p_done, PD["rep"])
            after()
            done(dve.tensor_tensor(tb[:, :], tb[:, :], node_ps[:, 0:L], ALU.mult))
            dve.wait_ge(p_done, PD["root"])
            after()
            done(dve.scalar_tensor_tensor(ta[:, :], hid_ps[:, 0:L], vec["bias"], tb[:, :], ALU.add, ALU.add), "conv_out")
            normed(PD["root"] + 1, "conv_sq", "conv_var", 1, ta[:, :], None)
            done(dve.tensor_scalar(ta[:, :], ta[:, :], vec["ln_w"], vec["ln_b"], ALU.mult, ALU.add))
            after()
            done(dve.tensor_tensor(ta[:, :], ta[:, :], x_col[:, :], ALU.add), "conv_pre")
            dve.wait_ge(a_done, 2)
            done(dve.tensor_tensor(ta[:, :], tb[:, :], x_col[:, :], ALU.add), "res1")
            normed(PD["root"] + 3, "res1_sq", "res1_var", 3, x1_col[:, :], "x1")
            dve.wait_ge(p_done, PD["x1_row"])
            for c, n in CHUNKS:
                done(dve.tensor_copy(x1_row[0:n, c // P, :], node_ps[0:n, c:c + P]), "x1_row" if n < P else None)

            after()
            in_form(dve, lambda: local_pass(lgin1, x1_row[:, :, :]), lambda: edge_pass(gin1))
            done(dve.tensor_scalar(tb[:, :], x1_col[:, :], vec["eps1"], None, ALU.mult))
            after()
            done(dve.tensor_tensor(tb[:, :], tb[:, :], x1_col[:, :], ALU.add))
            after()
            done(dve.tensor_tensor(ta[:, :], tb[:, :], acc[:, 0:L], ALU.add), "gin1_in")
            dve.wait_ge(a_done, A["h1"])
            done(dve.tensor_scalar(h1_col[:, :], h1_col[:, :], 0.0, None, ALU.max), "h1")
            dve.wait_ge(p_done, PD["h1_row"])
            for c, n in CHUNKS:
                done(dve.tensor_copy(h1_row[0:n, c // P, :], node_ps[0:n, c:c + P]), "h1_row" if n < P else None)

            after()
            in_form(dve, lambda: local_pass(lgin2, h1_row[:, :, :]), lambda: edge_pass(gin2))
            done(dve.tensor_scalar(tb[:, :], h1_col[:, :], vec["eps2"], None, ALU.mult))
            after()
            done(dve.tensor_tensor(tb[:, :], tb[:, :], h1_col[:, :], ALU.add))
            after()
            done(dve.tensor_tensor(ta[:, :], tb[:, :], acc[:, 0:L], ALU.add), "gin2_in")
            dve.wait_ge(p_done, PD["logits"])
            for c, n in CHUNKS:
                done(dve.tensor_tensor(y[0:n, 8 * (c // P):8 * (c // P) + 8, :],
                                       hid_ps[0:n, c:c + P].rearrange("p (h f) -> p h f", f=F),
                                       b2b_sb[0:n, :].rearrange("p (h f) -> p h f", f=F), ALU.add))
            after()

            def per_node(col):
                return col[:, :].unsqueeze(2).to_broadcast([P, 4 * H, F])

            done(dve.tensor_reduce(red[:, :], y[:, :, :], AX.X, ALU.max))
            after()
            done(dve.tensor_tensor(y[:, :, :], y[:, :, :], per_node(red), ALU.subtract), "shifted")
            dve.wait_ge(a_done, A["exp"])
            done(dve.tensor_reduce(red[:, :], y2[:, :, :], AX.X, ALU.add), "expsum")
            dve.wait_ge(a_done, A["ln"])
            done(dve.tensor_tensor(y[:, :, :], y[:, :, :], per_node(red2), ALU.subtract))
            after()
            done(dve.tensor_tensor(y[:, :, :], y[:, :, :], x1_row[:, :, :].rearrange("p c (h f) -> p (c h) f", f=F), ALU.add))
            after()
            done(dve.tensor_reduce(red[:, :], y[:, :, :], AX.X, ALU.add))
            after()
            done(dve.tensor_scalar(red[:, :], red[:, :], 1.0 / F, None, ALU.mult))
            after()
            done(dve.tensor_tensor(y[:, :, :], y[:, :, :], per_node(red), ALU.subtract))
            after()
            done(dve.tensor_tensor(y2[:, :, :], y[:, :, :], y[:, :, :], ALU.mult))
            after()
            done(dve.tensor_reduce(red[:, :], y2[:, :, :], AX.X, ALU.add))
            after()
            done(dve.tensor_scalar(red[:, :], red[:, :], 1.0 / F, EPS, ALU.mult, ALU.add), "out_var")
            dve.wait_ge(a_done, A["sqrt"])
            done(dve.reciprocal(red[:, :], red2[:, :]))
            after()
            done(dve.tensor_tensor(y[:, :, :], y[:, :, :], per_node(red), ALU.mult), "out")


SETUP_SPAN = 8
V = {"rep": 1, "rcnt": 3, "conv_out": 6, "conv_sq": 8, "conv_var": 9, "conv_pre": 13, "res1": 14,
     "res1_sq": 16, "res1_var": 17, "x1": 19, "x1_row": 23, "gin1_in": 26, "h1": 27, "h1_row": 31, "gin2_in": 34, 
     "shifted": 40, "expsum": 41, "out_var": 49, "out": 51}
A = {"conv_sqrt": 1, "conv_silu": 2, "res1_sqrt": 3, "gin1_mid": 4, "h1": 5, "gin2_mid": 6, "exp": 7, "ln": 8, "sqrt": 9}
PD = {"rep": 1, "root": 2, "x1_row": 7, "gin1_a": 8, "gin1_b": 9, "h1_row": 10, "gin2_a": 11, "logits": 12}


def kernel(**inputs):
    import numpy as np
    import concourse.bacc as bacc
    from concourse.bass_utils import run_bass_kernel_spmd

    a = {k: np.asarray(v) for k, v in inputs.items()}
    f32 = np.float32

    x_pad = np.zeros((L * H, F), f32)
    x_pad[:NODES] = a["x"]
    x_rows = x_pad.reshape(L, P)

    slots = GROUPS * TILES * P
    src = np.zeros(slots, np.int32)
    dst = np.full(slots, NODES, np.int32)
    src[:EDGES], dst[:EDGES] = a["src"], a["dst"]
    ids = np.concatenate([v.reshape(GROUPS, TILES, P).transpose(0, 2, 1) for v in (src, dst)], axis=2)

    ids_all = ids.transpose(1, 0, 2)
    bases = dst[::TILES * P].reshape(1, GROUPS)
    slot_bases = bases.reshape(UNITS, 2).T
    p = np.arange(P)
    columns = np.full((P, WHOLE + 4), -1.0, f32)
    for c in range(WHOLE):
        columns[:, c] = c * P + p
    columns[:SPLITS * REST, WHOLE] = WHOLE * P + p[:SPLITS * REST] % REST
    columns[:, WHOLE + 1], columns[:, WHOLE + 2], columns[:, WHOLE + 3] = p % WINDOW, 1.0, 0.0

    attr = np.zeros((slots, EDGE_F), f32)
    attr[:EDGES] = a["edge_attr_8"]
    attr = attr.reshape(GROUPS, 2, 2, 2, P, EDGE_F).transpose(0, 3, 5, 1, 2, 4).reshape(GROUPS, 2 * EDGE_F, 4 * P)

    def diagonal(w, n):
        out = np.zeros((n * w.shape[0], n * w.shape[1]), f32)
        for k in range(n):
            out[k * w.shape[0]:(k + 1) * w.shape[0], k * w.shape[1]:(k + 1) * w.shape[1]] = w
        return out

    w1 = diagonal(a["L0_gnn_W1"], 2)
    b1 = np.tile(a["L0_gnn_b1"], 2).reshape(P, 1)
    w2 = a["L0_gnn_W2"].reshape(HIDDEN, F, F).transpose(0, 2, 1).reshape(HIDDEN, F * F)
    w2 = diagonal(w2, 2)
    b2 = np.broadcast_to(a["L0_gnn_b2"].reshape(F, F).T.reshape(1, 1, F * F), (SPLITS, 2, F * F))
    mats = {"root": a["L0_gnn_root"], "w1a": a["L1_gnn_w1a"],
            "w1b": a["L1_gnn_w1b"], "w2a": a["L1_gnn_w2a"], "w2b": a["L1_gnn_w2b"],
            "mean": np.full((F, F), 1.0 / F, f32)}
    vecs = {"bias": a["L0_gnn_bias"], "ln_w": a["L0_gnn_ln_w"], "ln_b": a["L0_gnn_ln_b"], "b1a": a["L1_gnn_b1a"],
            "b1b": a["L1_gnn_b1b"], "b2a": a["L1_gnn_b2a"], "eps1": np.full(F, a["L1_gnn_eps1"]),
            "eps2": np.full(F, a["L1_gnn_eps2"])}
    arrays = {
        "x_rows": x_rows, "x_cols": x_rows.T, "ids": ids, "ids_all": ids_all,
        "src_rows": src.reshape(GROUPS, TILES * P), "bases": bases, "slot_bases": slot_bases, "edge_attr": attr, "w1": w1, "b1": b1, "w2": w2, "b2": b2,
        "mats": np.stack([diagonal(mats[n], H) for n in MATS], axis=1),
        "vecs": np.stack([np.tile(vecs[n], H) for n in VECS], axis=1),
        "b2b_row": np.broadcast_to(np.tile(a["L1_gnn_b2b"], H), (P, P)),
        "ident": np.eye(P, dtype=f32),
        "iota_cols": np.broadcast_to(np.arange(LP).astype(np.float16), (P, LP)),
        "slot_iota": np.broadcast_to(np.repeat(np.arange(WINDOW), UNIT).astype(np.float16), (P, WINDOW * UNIT)),
        "columns": columns,
    }
    arrays = {k: np.ascontiguousarray(v) for k, v in arrays.items()}
    nc = bacc.Bacc("TRN2", target_bir_lowering=False, num_devices=1)
    args = [nc.dram_tensor(f"in_{k}", v.shape, mybir.dt.from_np(v.dtype), kind="ExternalInput").ap()
            for k, v in arrays.items()]
    out = nc.dram_tensor("out_0", (NODES, F), mybir.dt.float32, kind="ExternalOutput").ap()
    gnn_kernel(nc, *args, out)
    r = run_bass_kernel_spmd(nc, [{f"in_{k}": v for k, v in arrays.items()}], core_ids=[0])
    return r.results[0]["out_0"]
```

```python
import concourse.bass as bass
from concourse import mybir
from contextlib import ExitStack

NODES, F, EDGES = 3125, 16, 103125
EDGE_F, HIDDEN = 8, 64
P = 128
H = P // F
H_BITS = 3
L = -(-NODES // H)
LP = L + L % 2
TILES = 8
UNIT = 2 * TILES
UNITS = -(-EDGES // (P * UNIT))
GROUPS = 2 * UNITS
WINDOW = P // 2
DMA_CONV, DMA_GIN = 12, 6
ONEHOT = UNIT - DMA_GIN
WHOLE = L // P
REST = L - WHOLE * P
TURN = 3
TURNS = UNITS // TURN
TURN_L = L // TURNS
AHEAD = 4
REACH = 64
MARGIN = (REACH - TURN_L) // 2
HALVES = (slice(0, UNITS // 2), slice(UNITS // 2, UNITS))
BANK = 512
CHUNKS = [(c, min(P, L - c)) for c in range(0, L, P)]
SPLITS = 3
VECS = ["b1a", "b1b", "b2a", "eps1", "eps2"]
MATS = ["root", "w1a", "w1b", "w2a", "w2b"]
ROWS = ["bias", "ln_w", "ln_b", "b2b"]
EPS = 1e-5
CONSTANTS = 10
assert H == 1 << H_BITS and UNITS % 2 == 1 and UNITS == TURN * TURNS and L == TURN_L * TURNS and SPLITS * REST <= P
assert DMA_CONV == 12
assert REACH == WINDOW and TURN_L * (TURNS - 1) + REACH <= BANK


def gnn_kernel(nc, x_rows, x_cols, ids, ids_all, src_rows, bases, slot_bases, first_cols, edge_attr, w1, b1, w2, b2, b2_mat, mats, vecs,
               row_vecs, ident, iota_cols, slot_iota, columns, out):
    f32, bf16, f16, i32 = mybir.dt.float32, mybir.dt.bfloat16, mybir.dt.float16, mybir.dt.int32
    ALU, ACT, AX = mybir.AluOpType, mybir.ActivationFunctionType, mybir.AxisListType

    ctx = ExitStack()
    with ctx:
        def sb(name, shape, dt):
            return ctx.enter_context(nc.sbuf_tensor(name, shape, dt))

        def ps(name, shape, dt=f32):
            return ctx.enter_context(nc.psum_tensor(name, shape, dt))

        def sem(name):
            return ctx.enter_context(nc.semaphore(name))

        table_xy = nc.dram_tensor("table_xy", (L * H, 2 * F), f32, kind="Internal").ap()
        table_x1 = nc.dram_tensor("table_x1", (L * H, F), f32, kind="Internal").ap()
        l_rows = nc.dram_tensor("l_rows", (UNITS, UNIT * P), f16, kind="Internal").ap()
        table_h1 = nc.dram_tensor("table_h1", (L * H, F), f32, kind="Internal").ap()

        def scope():
            stack = ctx.enter_context(ExitStack())
            return stack, lambda name, shape, dt: stack.enter_context(nc.sbuf_tensor(name, shape, dt))

        stack, early = scope()
        ids_all_sb = early("ids_all_sb", [P, GROUPS, 2 * TILES], i32)
        src_rows_sb = early("src_rows_sb", [GROUPS, P * TILES], i32)
        src_l_rows = early("src_l_rows", [GROUPS, P * TILES], f16)
        src_h_sb = early("src_h_sb", [P, GROUPS, TILES], i32)
        local_dst = early("local_dst", [P, GROUPS, TILES], f32)
        stack.close()
        slot_l = sb("slot_l", [P, UNITS, REACH], bf16)
        slot_hf = sb("slot_hf", [P, UNITS, H, F], bf16)
        hot_l = [sb(f"hot_l{s}", [P, TILES, LP], bf16) for s in range(2)]

        stack, early = scope()
        slot_v = early("slot_v", [P, UNITS, F], f32)
        slot_left1 = early("slot_left1", [P, UNITS, F], f32)
        slot_left2 = early("slot_left2", [P, UNITS, F], f32)
        slot_parts = early("slot_parts", [P, UNITS, SPLITS, F], bf16)
        slot_spread = [early(f"slot_spread{b}", [P, TURN, SPLITS, H, F], bf16) for b in range(AHEAD)]
        slot_cnt = early("slot_cnt", [P, UNITS, H], f16)
        stack.close()
        prod = [sb(f"prod{q}", [P, 4, F, F], f32) for q in range(2)]
        src_hot = [sb(f"src_hot{s}", [P, WHOLE + 1, ONEHOT * P], bf16) for s in range(2)]
        picked = sb("picked", [P, ONEHOT, H, F], f32)

        w1_sb = sb("w1_sb", [2 * EDGE_F, P], f32)
        b1_sb = sb("b1_sb", [P, 1], f32)
        w2_sb = sb("w2_sb", [P, 2 * F * F], f32)
        b2_sb = sb("b2_sb", [SPLITS, 2, F * F], f32)
        b2_left = sb("b2_left", [SPLITS, 2, 2, F * F], f32)
        b2_part = sb("b2_part", [SPLITS, SPLITS - 1, 2, F * F], bf16)
        b2_rows = sb("b2_rows", [P, 2, F * F], bf16)
        ones_sb = sb("ones_sb", [P, P], bf16)
        mats_sb = sb("mats_sb", [P, len(MATS), P], f32)
        vecs_sb = sb("vecs_sb", [P, len(VECS)], f32)
        row_vecs_sb = sb("row_vecs_sb", [P, len(ROWS), H, F], f32)
        row_vec = {n: row_vecs_sb[:, k, :, :] for k, n in enumerate(ROWS)}
        one_row = sb("one_row", [1, P], f32)
        ident_sb = sb("ident_sb", [P, P], f32)
        iota_l = sb("iota_l", [P, LP], f16)
        slot_iota_sb = sb("slot_iota_sb", [P, WINDOW * UNIT], f16)
        columns_sb = sb("columns_sb", [P, WHOLE + 3], f32)
        col_slot, col_one = columns_sb[:, WHOLE + 1:WHOLE + 2], columns_sb[:, WHOLE + 2:WHOLE + 3]
        iota_h = iota_l[:, 0:H]
        zero_sb = sb("zero_sb", [P, BANK], bf16)
        mat = {n: mats_sb[:, k, :] for k, n in enumerate(MATS)}
        vec = {n: vecs_sb[:, k:k + 1] for k, n in enumerate(VECS)}

        ids_sb = [sb(f"ids{s}", [P, 2, 2 * TILES], i32) for s in range(2)]
        ea_sb = [sb(f"ea{s}", [2 * EDGE_F, 2, P * TILES // 2], f32) for s in range(2)]
        hid_sb = [sb(f"hid{s}", [P, 2, P * TILES // 2], f32) for s in range(2)]
        rows = [sb(f"rows{s}", [P, UNIT, 3 * F], f32) for s in range(2)]
        rest1 = sb("rest1", [P, UNIT, F], f32)
        rest2 = sb("rest2", [P, UNIT, F], f32)

        dst_h = sb("dst_h", [P, TILES], i32)
        dst_l = sb("dst_l", [P, TILES], i32)
        dst_hf = sb("dst_hf", [P, TILES], f32)
        dst_lf = sb("dst_lf", [P, TILES], f32)
        hot_h = [sb(f"hot_h{s}", [P, TILES, H], bf16) for s in range(2)]
        msg = sb("msg", [P, TILES, F], f32)
        part = [sb(f"part{k}", [P, TILES, F], bf16) for k in range(SPLITS)]
        spread = [src_hot[s][:, :, :].rearrange("p a b -> p (a b)")[:, 0:SPLITS * TILES * P].rearrange(
            "p (k t h f) -> p k t h f", k=SPLITS, t=TILES, h=H) for s in range(2)]

        bases_sb = sb("bases_sb", [P, GROUPS], i32)
        slot_bases_sb = sb("slot_bases_sb", [P, UNITS], i32)
        local16 = sb("local16", [P, UNITS, UNIT], f16)
        masks = sb("masks", [P, UNITS, ONEHOT, H], bf16)
        span = sb("span", [P, 5], f32)
        first_l = sb("first_l", [P, UNITS], f32)
        is_local = sb("is_local", [1, 1], i32)
        slot_n = sb("slot_n", [P, UNITS], i32)
        slot_ni = sb("slot_ni", [P, UNITS], i32)
        slot_rel = sb("slot_rel", [P, UNITS], f32)
        slot_neg = sb("slot_neg", [P, UNITS], f32)
        slot_h = sb("slot_h", [P, UNITS, H], bf16)
        slot_tmp = sb("slot_tmp", [P, REACH], bf16)
        distance = sb("distance", [P, WHOLE + 1, (UNIT - DMA_CONV) * P], f16)
        src_l_b = [sb(f"src_l_b{s}", [P, ONEHOT * P], f16) for s in range(2)]
        table_parts = sb("table_parts", [P, WHOLE + 1, SPLITS, P], bf16)
        table_rest = sb("table_rest", [P, P], bf16)
        parts = [sb(f"parts{s}", [P, UNIT, SPLITS * F + 2], bf16) for s in range(2)]
        dst_hot = [sb(f"dst_hot{s}", [P, WINDOW, UNIT], bf16) for s in range(2)]
        sums = sb("sums", [P, UNITS, SPLITS * F + 1], f32)

        x_row = sb("x_row", [P, 4, H, F], f32)
        xy_row = sb("xy_row", [P, 4, H, 2, F], f32)
        b2_mat_sb = sb("b2_mat_sb", [P, P], f32)
        x_col = sb("x_col", [P, L], f32)
        x1_col = sb("x1_col", [P, L], f32)
        x1_row = sb("x1_row", [P, 4, P], f32)
        h1_col = sb("h1_col", [P, L], f32)
        h1_row = sb("h1_row", [P, 4, P], f32)
        ta = sb("ta", [P, L], f32)
        tb = sb("tb", [P, L], f32)
        edges_in = sb("edges_in", [H, L], f32)
        y = sb("y", [P, 4 * H, F], f32)
        y2 = sb("y2", [P, 4 * H, F], f32)
        red = sb("red", [P, 4 * H], f32)
        red2 = sb("red2", [P, 4 * H], f32)

        bank = ps("bank", [P, 8, 512])
        hid_ps, we_ps, node_ps = bank[:, 2, :], bank[:, 3:7, :], bank[:, 7, :]
        acc, cnt = bank[:, 0, MARGIN:MARGIN + L], bank[:, 1, MARGIN:MARGIN + L]

        def local_ps(e, s):
            return bank[:, 1, P * s:P * s + P] if e.mlp else bank[:, s, 0:P]

        def gather_bank(e, s):
            return 7 * s if e.mlp else 2 + 3 * s

        consts_in = sem("consts_in")
        x_in = sem("x_in")
        ids_all_in = sem("ids_all_in")
        slot_bases_in = sem("slot_bases_in")
        src_rows_in = sem("src_rows_in")
        consts_ready = sem("consts_ready")
        table_in = sem("table_in")
        v_done = sem("v_done")
        a_done = sem("a_done")
        p_done = sem("p_done")
        out_done = sem("out_done")
        zeroed = sem("zeroed")
        setup = sem("setup")
        span_sum = sem("span_sum")
        form_known = sem("form_known")
        x_col_in = sem("x_col_in")
        xy_made = sem("xy_made")
        xy_ready = sem("xy_ready")
        xy_in = sem("xy_in")
        src_l_ready = sem("src_l_ready")
        l_rows_in = sem("l_rows_in")
        hot_steps = sem("hot_steps")
        slot_hots = sem("slot_hots")
        slots_added = sem("slots_added")
        slot_cnt_made = sem("slot_cnt_made")
        slot_part = [sem(f"slot_part{n}") for n in range(SPLITS)]
        slot_left = [sem(f"slot_left{n}") for n in range(SPLITS - 1)]
        sums_done = [sem(f"sums_done{k}") for k in range(3)]

        class Local:
            def __init__(self, name, mlp, by_dma, summed, halves):
                self.mlp, self.by_dma, self.summed = mlp, by_dma, summed
                self.halves = halves
                self.onehot = UNIT - by_dma
                self.ids_in = [sem(f"{name}_ids_in{s}") for s in range(2)]
                self.l_in = [sem(f"{name}_l_in{s}") for s in range(2)]
                self.rows_in = [sem(f"{name}_rows_in{s}") for s in range(2)]
                self.rows_used = sem(f"{name}_rows_used")
                self.turns = sem(f"{name}_turns")
                self.src_hots = [sem(f"{name}_src_hots{s}") for s in range(2)]
                self.gathered = [sem(f"{name}_gathered{s}") for s in range(2)]
                self.picks = [sem(f"{name}_picks{s}") for s in range(2)]
                self.chain = sem(f"{name}_chain")
                self.values = sem(f"{name}_values")
                self.part1 = sem(f"{name}_part1")
                self.rest1 = sem(f"{name}_rest1")
                self.part2 = sem(f"{name}_part2")
                self.rest2 = sem(f"{name}_rest2")
                self.part3 = sem(f"{name}_part3")
                self.dst_hots = sem(f"{name}_dst_hots")
                self.summed_unit = [sem(f"{name}_summed_unit{s}") for s in range(2)]
                self.stored = sem(f"{name}_stored")
                self.table = sem(f"{name}_table")
                self.table_steps = sem(f"{name}_table_steps")
                self.table_rest = sem(f"{name}_table_rest")
                self.spreads = [sem(f"{name}_slot_spreads{b}") for b in range(AHEAD)]
                self.spreads_used = [sem(f"{name}_slot_spreads_used{b}") for b in range(AHEAD)]
                if mlp:
                    self.ea_in = [sem(f"{name}_ea_in{s}") for s in range(2)]
                    self.hid_made = sem(f"{name}_hid_made")
                    self.silu = [sem(f"{name}_silu{s}") for s in range(2)]
                    self.we_made = [sem(f"{name}_we_made{b}") for b in range(2)]
                    self.we_read = [sem(f"{name}_we_read{b}") for b in range(2)]
                    self.chosen = sem(f"{name}_chosen")
                    self.reduced = sem(f"{name}_reduced")

        class Edges:
            def __init__(self, name, local):
                self.mlp, self.summed = local.mlp, local.summed
                self.ids_in, self.rows_in, self.turns, self.hots, self.vec = (
                    local.ids_in, local.rows_in, local.turns, local.src_hots, local.chain)
                self.ids_used, self.spreads = [local.part1, local.part2], [local.rest1, local.rest2]
                self.rows_used, self.scattered = local.picks, local.summed_unit
                if self.mlp:
                    self.ea_in, self.silu, self.hid_made = local.ea_in, local.silu, local.hid_made
                    self.we_read = local.we_read
                    self.hid_read = sem(f"{name}_hid_read")
                    self.we_made = [[sem(f"{name}_we_made{q}{s}") for s in range(2)] for q in range(2)]

        lconv, lgin1, lgin2 = (Local(n, n == "conv", DMA_CONV if n == "conv" else DMA_GIN, d, 2 * k)
                               for k, (n, d) in enumerate(zip(("conv", "gin1", "gin2"), sums_done)))
        conv, gin1, gin2 = (Edges(f"general_{n}", l) for n, l in (("conv", lconv), ("gin1", lgin1), ("gin2", lgin2)))

        def pairs(eng, step, first=0, last=GROUPS // 2):
            with eng.Fori(first, last) as i:
                for s in range(2):
                    step(2 * i + s, i, s)

        def next_of(u, i, s):
            return u + 1, (i + 1 if s else i), 1 - s

        def row_blocks(table, rows):
            yield table[0:WHOLE * P, :].rearrange("(c p) n -> p c n", p=P), rows[:, 0:WHOLE, :]
            yield table[WHOLE * P:L, :], rows[0:REST, WHOLE, :]

        def second_of(u, i, s):
            return u + 2, i + 1, s

        def last_of(u, i, s):
            return u - 1, (i if s else i - 1), 1 - s

        def is_first(u):
            return isinstance(u, int) and u == 0

        def all_units(eng, step):
            for s in range(2):
                step(s, 0, s, 2)
            pairs(eng, lambda u, i, s: step(u, i, s, 2), first=1, last=UNITS // 2 - 1)
            for u in range(UNITS - 3, UNITS):
                step(u, u // 2, u % 2, UNITS - 1 - u)

        def all_turns(eng, step, first=0):
            with eng.Fori(first, TURNS // AHEAD) as i:
                for b in range(AHEAD):
                    step(AHEAD * i + b, i, b)
            for b in range(TURNS % AHEAD):
                step(TURNS // AHEAD * AHEAD + b, TURNS // AHEAD, b)

        def in_form(eng, local, general):
            with eng.If(form[eng.engine]):
                local()
            with eng.Else():
                general()

        form = {}

        def learn_form(eng):
            eng.wait_ge(form_known, 1)
            form[eng.engine] = eng.value_load(is_local[0:1, 0:1], min_val=0, max_val=1)

        block = ctx.enter_context(nc.Block())

        @block.sync
        def _(sp):
            sp.dma_start(ids_all_sb[:, :, :], ids_all).then_inc(ids_all_in, 16)
            sp.dma_start(bases_sb[:, :], bases.to_broadcast([P, GROUPS])).then_inc(ids_all_in, 16)
            sp.dma_start(columns_sb[:, :], columns).then_inc(ids_all_in, 16)
            for k in range(2):
                sp.dma_start(slot_bases_sb[WINDOW * k:WINDOW * k + WINDOW, :],
                             slot_bases[k:k + 1, :].to_broadcast([WINDOW, UNITS])).then_inc(slot_bases_in, 16)
            sp.dma_start(first_l[:, :], first_cols.to_broadcast([P, UNITS])).then_inc(slot_bases_in, 16)
            sp.dma_start(x_col[:, :], x_cols).then_inc(x_col_in, 16)
            sp.dma_start(b2_mat_sb[:, :], b2_mat).then_inc(x_col_in, 16)
            sp.dma_start(src_rows_sb[:, :], src_rows).then_inc(src_rows_in, 16)
            sp.wait_ge(zeroed, 1)
            for dram, row in row_blocks(x_rows, x_row[:, :, :, :].rearrange("p c h f -> p c (h f)")):
                sp.dma_start(row, dram).then_inc(x_in, 16)
            loads = [(iota_l[:, :], iota_cols), (w1_sb[:, :], w1), (b1_sb[:, :], b1), (slot_iota_sb[:, :], slot_iota),
                     (ident_sb[:, :], ident), (b2_sb[:, :, :], b2), (w2_sb[:, :], w2),
                     (mats_sb[:, :, :], mats), (vecs_sb[:, :], vecs), (row_vecs_sb[:, :, :, :], row_vecs)]
            assert len(loads) == CONSTANTS
            for dst, src in loads:
                sp.dma_start(dst, src).then_inc(consts_in, 16)
            sp.wait_ge(src_l_ready, 1)
            sp.dma_start(l_rows.rearrange("u (g n) -> (u g) n", g=2), src_l_rows[:, :]).then_inc(l_rows_in, 16)
            learn_form(sp)

            def write_table(table, rows, done):
                sp.wait_ge(v_done, done)
                for dram, row in row_blocks(table.rearrange("(l h) f -> l (h f)", h=H), rows):
                    sp.dma_start(dram, row).then_inc(table_in, 16)

            def feed(e, table=()):
                if e.mlp:
                    sp.wait_ge(l_rows_in, 16)
                if table:
                    write_table(*table)

                def load(g, i, s, fresh=False):
                    if not fresh:
                        sp.wait_ge(e.rows_in[s], 16 * TILES * i)
                        sp.wait_ge(e.ids_used[s], i)
                    sp.dma_start(ids_sb[s][:, 0, :], ids[bass.ds(g, 1), :, :].rearrange("o p n -> p (o n)")).then_inc(e.ids_in[s], 16)
                    if e.mlp:
                        if not fresh:
                            sp.wait_ge(e.silu[s], i)
                        sp.dma_start(ea_sb[s][:, 0, :], edge_attr[bass.ds(g, 1), :, :].rearrange("o k n -> k (o n)")).then_inc(e.ea_in[s], 16)
                for g in range(2):
                    load(g, 0, g, fresh=True)
                pairs(sp, load, first=1)

            def feed_local(e, last=None, table=()):
                def load_l(u, s):
                    sp.dma_start(src_l_b[s][:, 0:e.onehot * P],
                                 l_rows[bass.ds(u, 1), e.by_dma * P:].to_broadcast([P, e.onehot * P])).then_inc(e.l_in[s], 16)

                def load_ids(u, s):
                    sp.dma_start(ids_sb[s][:, :, :], ids[bass.ds(2 * u, 2), :, :].rearrange("g p n -> p g n")).then_inc(e.ids_in[s], 16)

                def load_attributes(u, s):
                    sp.dma_start(ea_sb[s][:, :, :], edge_attr[bass.ds(2 * u, 2), :, :].rearrange("g k n -> k g n")).then_inc(e.ea_in[s], 16)

                def load(u, i, s):
                    sp.wait_ge(e.src_hots[s], i)
                    load_l(u, s)
                    sp.wait_ge(e.rows_in[s], 16 * e.by_dma * i)
                    load_ids(u, s)
                    if e.mlp:
                        sp.wait_ge(e.silu[s], 2 * i)
                        load_attributes(u, s)

                if last:
                    sp.wait_ge(last.summed, 1)
                else:
                    sp.wait_ge(xy_ready, 1)
                    for dram, row in row_blocks(table_xy.rearrange("(l h) f -> l (h f)", h=H),
                                                xy_row[:, :, :, :, :].rearrange("p c h t f -> p c (h t f)")):
                        sp.dma_start(dram, row).then_inc(xy_in, 16)
                for s in range(2):
                    load_ids(s, s)
                if e.mlp:
                    for s in range(2):
                        load_attributes(s, s)
                    sp.wait_ge(l_rows_in, 16)
                for s in range(2):
                    load_l(s, s)
                if table:
                    write_table(*table)
                sp.wait_ge(e.table, 1)
                for k in range(SPLITS):
                    sp.dma_start(table_rest[REST * k:REST * k + REST, :], table_parts[0:REST, WHOLE, k, :]).then_inc(e.table_rest, 16)
                pairs(sp, load, first=1, last=UNITS // 2)
                load(UNITS - 1, UNITS // 2, 0)

            in_form(sp, lambda: feed_local(lconv), lambda: feed(conv))
            for last, local, general, write in ((lconv, lgin1, gin1, (table_x1, x1_row, V["x1_row"])),
                                                (lgin1, lgin2, gin2, (table_h1, h1_row, V["h1_row"]))):
                in_form(sp, lambda: feed_local(local, last, write), lambda: feed(general, write))
            sp.wait_ge(v_done, V["out"])
            y_rows = y[:, :, :].rearrange("p (c h) f -> p c (h f)", h=H)
            o_flat = out.rearrange("n f -> (n f)")
            full = NODES // H
            sp.dma_start(o_flat[0:WHOLE * P * P].rearrange("(c l k) -> l c k", l=P, k=P), y_rows[:, 0:WHOLE, :]).then_inc(out_done, 16)
            m = full - WHOLE * P
            sp.dma_start(o_flat[WHOLE * P * P:full * P].rearrange("(l k) -> l k", k=P), y_rows[0:m, WHOLE, :]).then_inc(out_done, 16)
            tail = (NODES - full * H) * F
            sp.dma_start(o_flat[full * P:NODES * F].rearrange("(o k) -> o k", o=1), y_rows[m:m + 1, WHOLE, 0:tail]).then_inc(out_done, 16)
            sp.wait_ge(out_done, 16 * 3)

        @block.gpsimd
        def _(pool):
            learn_form(pool)

            def gather(e, table):
                def step(g, i, s):
                    pool.wait_ge(e.ids_in[s], 16 * (i + 1))
                    pool.wait_ge(e.rows_used[s], i + 1)
                    pool.sem_inc(e.turns, 1)
                    for t in range(TILES):
                        pool.indirect_dma_start(
                            out=rows[s][:, t, F:2 * F], out_offset=None, in_=table,
                            in_offset=bass.IndirectOffsetOnAxis(ap=ids_sb[s][:, 0, t:t + 1], axis=0),
                        ).then_inc(e.rows_in[s], 16)
                pairs(pool, step)

            def gather_local(e, table):
                if e.mlp:
                    table = table_xy
                    pool.wait_ge(xy_in, 16 * 2)

                def step(u, i, s, more):
                    pool.wait_ge(e.ids_in[s], 16 * (i + 1))
                    pool.wait_ge(e.rows_used, u + 1)
                    pool.sem_inc(e.turns, 1)
                    for t in range(e.by_dma):
                        pool.indirect_dma_start(
                            out=rows[s][:, t, F:3 * F if e.mlp else 2 * F], out_offset=None, in_=table,
                            in_offset=bass.IndirectOffsetOnAxis(ap=ids_sb[s][:, t // TILES, t % TILES:t % TILES + 1], axis=0),
                        ).then_inc(e.rows_in[s], 16)
                all_units(pool, step)

            table_x = x_rows.rearrange("l (h f) -> (l h) f", f=F)
            for n, (local, general, tab) in enumerate(((lconv, conv, table_x), (lgin1, gin1, table_x1), (lgin2, gin2, table_h1))):
                if n:
                    pool.wait_ge(table_in, 16 * 2 * n)
                in_form(pool, lambda: gather_local(local, tab), lambda: gather(general, tab))

        @block.tensor
        def _(pe):
            for e in (lconv, lgin1, lgin2):
                for s in range(2):
                    pe.sem_inc(e.gathered[s], 1)
                    pe.sem_inc(e.summed_unit[s], 1)
                for b in range(AHEAD):
                    pe.sem_inc(e.spreads_used[b], 1)
            pe.sem_inc(lconv.we_made[1], 3)
            for q in range(2):
                for s in range(2):
                    pe.sem_inc(conv.we_made[q][s], 1)
            def scatter(e, i, s):
                pe.wait_ge(e.hots[s], i + 1)
                pe.wait_ge(e.spreads[s], i + 1)
                for t in range(TILES):
                    for k in range(SPLITS):
                        mm = pe.matmul(acc, spread[s][:, k, t, :, :].rearrange("p h f -> p (h f)"),
                                       hot_l[s][:, t, 0:L], start=False, stop=False, skip_group_check=True)
                    if e.mlp:
                        mm = pe.matmul(cnt[0:H, :], hot_h[s][:, t, :], hot_l[s][:, t, 0:L],
                                       start=False, stop=False, skip_group_check=True)
                mm.then_inc(e.scattered[s], 1)

            def open_sums(e):
                pe.matmul(bank[:, 0, :], zero_sb[:, 0:P], zero_sb[:, :], start=True, stop=False, skip_group_check=True)
                if e.mlp:
                    pe.matmul(bank[0:H, 1, :], zero_sb[:, 0:H], zero_sb[:, :], start=True, stop=False, skip_group_check=True)

            def close_sums(e):
                mm = pe.matmul(bank[:, 0, :], zero_sb[:, 0:P], zero_sb[:, :], start=False, stop=True, skip_group_check=True)
                if e.mlp:
                    mm = pe.matmul(bank[0:H, 1, :], zero_sb[:, 0:H], zero_sb[:, :], start=False, stop=True, skip_group_check=True)
                mm.then_inc(e.summed, 1)

            def weights_of(hid, q, with_b2=True):
                for k in range(2):
                    if with_b2:
                        pe.matmul(we_ps[:, 2 * q + k, :], ones_sb[:, :], b2_rows[:, :, :].rearrange("p k n -> p (k n)"),
                                  start=True, stop=False, skip_group_check=True)
                    mm = pe.matmul(we_ps[:, 2 * q + k, :], hid[:, P * (2 * q + k):P * (2 * q + k) + P], w2_sb[:, :],
                                   start=not with_b2, stop=True, skip_group_check=True)
                return mm

            def hidden(g, i, s):
                pe.wait_ge(conv.ea_in[s], 16 * (i + 1))
                pe.wait_ge(conv.hid_read, g + 1)
                pe.matmul(hid_ps, w1_sb[:, :], ea_sb[s][:, 0, :], start=True, stop=True).then_inc(conv.hid_made, 1)

            def edge_weights(g, i, s):
                pe.wait_ge(conv.silu[s], i + 1)
                for q in range(2):
                    pe.wait_ge(conv.we_read[q], g + 1)
                    weights_of(hid_sb[s][:, 0, :], q).then_inc(conv.we_made[q][s], 1)

            pe.wait_ge(x_col_in, 16 * 2)
            for c, n in CHUNKS:
                mm = pe.matmul(hid_ps[0:n, c:c + P], x_col[:, c:c + n], b2_mat_sb[:, :], start=True, stop=True)
            mm.then_inc(xy_made, 1)
            pe.wait_ge(setup, SETUP_SPAN)
            pe.matmul(node_ps[0:1, 0:1], span[:, 4:5], col_one, start=True, stop=True).then_inc(span_sum, 1)
            learn_form(pe)

            def gather_onehot(e, u, i, s):
                pe.wait_ge(e.src_hots[s], i + 1)
                pe.wait_ge(e.picks[s], i + 1)
                first = gather_bank(e, s)
                def tile_bank(t):
                    return bank[:, first + t // 4, P * (t % 4):P * (t % 4) + P]

                def whole_chunks(t):
                    for c in range(WHOLE):
                        for k in range(SPLITS):
                            pe.matmul(tile_bank(t), src_hot[s][:, c, P * t:P * t + P], table_parts[:, c, k, :],
                                      start=(t % 4 == 0 and c == 0 and k == 0), stop=False, skip_group_check=True)

                def last_chunk(t):
                    return pe.matmul(tile_bank(t), src_hot[s][:, WHOLE, P * t:P * t + P], table_rest[:, :],
                                     start=False, stop=True, skip_group_check=True)

                if is_first(u):
                    for t in range(e.onehot):
                        whole_chunks(t)
                    pe.wait_ge(e.table_rest, 16 * SPLITS)
                    for t in range(e.onehot):
                        mm = last_chunk(t)
                else:
                    for t in range(e.onehot):
                        whole_chunks(t)
                        mm = last_chunk(t)
                mm.then_inc(e.gathered[s], 1)

            def sum_unit(e, u, i, s):
                pe.wait_ge(e.part3, u + 2)
                pe.wait_ge(e.dst_hots, u + 1)
                pe.wait_ge(e.stored, u + (2 if e.mlp else 1))
                n = SPLITS * F + (1 if e.mlp else 0)
                for g in range(2):
                    for t in range(TILES):
                        mm = pe.matmul(local_ps(e, s)[WINDOW * g:WINDOW * g + WINDOW, 0:n], dst_hot[s][:, :, TILES * g + t],
                                       parts[s][:, TILES * g + t, 0:n], start=(t == 0), stop=(t == TILES - 1))
                mm.then_inc(e.summed_unit[s], 1)

            def hidden_local(u, i, s, k):
                if k == 0:
                    pe.wait_ge(lconv.ea_in[s], 16 * (i + 1))
                    if not is_first(u):
                        pe.wait_ge(lconv.silu[1 - s], 2 * (i + s))
                else:
                    pe.wait_ge(lconv.silu[s], 2 * i + 1)
                pe.matmul(hid_ps, w1_sb[:, :], ea_sb[s][:, k, :], start=True, stop=True).then_inc(lconv.hid_made, 1)

            def edge_weights_local(u, i, s, quads):
                pe.wait_ge(lconv.silu[s], 2 * i + quads[0] // 2 + 1)
                for q in quads:
                    pe.wait_ge(lconv.we_read[q % 2], 2 * u + q // 2 + 1)
                    weights_of(hid_sb[s][:, q // 2, :], q % 2, with_b2=4 * q >= DMA_CONV).then_inc(lconv.we_made[q % 2], 1)

            def local_pass(e):
                if e.mlp:
                    pe.wait_ge(consts_in, 16 * CONSTANTS)
                    pe.wait_ge(xy_ready, 1)
                    hidden_local(0, 0, 0, 0)
                    edge_weights_local(0, 0, 0, (0, 1))
                pe.wait_ge(e.table, 1)
                gather_onehot(e, 0, 0, 0)
                if e.mlp:
                    hidden_local(0, 0, 0, 1)
                    pe.wait_ge(consts_ready, 1)
                    hidden_local(1, 0, 1, 0)
                else:
                    gather_onehot(e, 1, 0, 1)

                def step(u, i, s, more):
                    if e.mlp:
                        edge_weights_local(u, i, s, (2, 3))
                        if is_first(u):
                            gather_onehot(e, 1, 0, 1)
                            hidden_local(1, 0, 1, 1)
                        if more:
                            edge_weights_local(*next_of(u, i, s), (0, 1))
                        if more == 2:
                            hidden_local(*second_of(u, i, s), 0)
                    if not is_first(u):
                        sum_unit(e, *last_of(u, i, s))
                    if more == 2:
                        gather_onehot(e, *second_of(u, i, s))
                        if e.mlp:
                            hidden_local(*second_of(u, i, s), 1)
                all_units(pe, step)
                sum_unit(e, UNITS - 1, UNITS // 2, 0)
                pe.wait_ge(e.stored, UNITS + 2)
                open_sums(e)
                if e.mlp:
                    pe.wait_ge(slot_cnt_made, 1)

                def scatter_turn(t, i, b):
                    pe.wait_ge(e.spreads[b], i + 1)
                    for j in range(TURN):
                        unit = bass.ds(TURN * t + j, 1)
                        reach = bass.ds(TURN_L * t, REACH)
                        cols_l = slot_l[:, unit, :].rearrange("p o l -> p (o l)")
                        if e.mlp:
                            pe.matmul(bank[0:H, 1, reach], slot_cnt[:, unit, :].rearrange("p o h -> p (o h)"), cols_l,
                                      start=False, stop=False, skip_group_check=True)
                        for k in range(SPLITS):
                            mm = pe.matmul(bank[:, 0, reach], slot_spread[b][:, j, k, :, :].rearrange("p h f -> p (h f)"), cols_l,
                                           start=False, stop=False, skip_group_check=True)
                    mm.then_inc(e.spreads_used[b], 1)

                all_turns(pe, scatter_turn)
                close_sums(e)

            def conv_step(g, i, s):
                hidden(g, i, s)
                scatter(conv, i - 1, s)
                edge_weights(g, i, s)

            def general_conv():
                pe.wait_ge(xy_ready, 1)
                pe.wait_ge(consts_ready, 1)
                open_sums(conv)
                for g in range(2):
                    hidden(g, 0, g)
                    edge_weights(g, 0, g)
                pairs(pe, conv_step, first=1)
                for s in range(2):
                    scatter(conv, GROUPS // 2 - 1, s)
                close_sums(conv)

            in_form(pe, lambda: local_pass(lconv), general_conv)

            def cols(dst, weights, src, v):
                pe.wait_ge(v_done, v)
                pe.matmul(dst, weights, src, start=True, stop=True).then_inc(p_done, 1)

            def acols(dst, weights, src, a):
                pe.wait_ge(a_done, a)
                pe.matmul(dst, weights, src, start=True, stop=True).then_inc(p_done, 1)

            def to_rows(dst, src):
                for c, n in CHUNKS:
                    mm = pe.transpose(dst[0:n, c:c + P], src[:, c:c + n], ident_sb[:, :])
                mm.then_inc(p_done, 1)

            node, big = node_ps[:, 0:L], bank[:, 2, 0:L]
            for c, n in CHUNKS:
                pe.matmul(hid_ps[0:n, c:c + P], x_col[:, c:c + n], mat["root"], start=True, stop=False)
                mm = pe.matmul(hid_ps[0:n, c:c + P], one_row[:, 0:n], row_vecs_sb[0:1, 0, :, :].rearrange("p h f -> p (h f)"),
                               start=False, stop=True)
            mm.then_inc(p_done, 1)
            pe.wait_ge(v_done, V["edges_in"])
            for c, n in CHUNKS:
                pe.transpose(bank[0:n, 3, H * (c // P):H * (c // P) + H], edges_in[:, c:c + n], ident_sb[0:H, 0:H])
            to_rows(node_ps, tb)
            pe.wait_ge(v_done, V["x1_row"])
            for c, n in CHUNKS:
                mm = pe.transpose(node_ps[:, c:c + n], x1_row[0:n, c // P, :], ident_sb[0:n, 0:n])
            mm.then_inc(p_done, 1)
            pe.wait_ge(a_done, A["x1_col"])

            def gin(e):
                open_sums(e)
                pairs(pe, lambda g, i, s: scatter(e, i, s))
                close_sums(e)

            in_form(pe, lambda: local_pass(lgin1), lambda: gin(gin1))
            cols(node, mat["w1a"], ta[:, :], V["gin1_in"])
            acols(big, mat["w1b"], tb[:, :], A["gin1_mid"])
            pe.wait_ge(a_done, A["h1"])
            to_rows(node_ps, h1_col)
            in_form(pe, lambda: local_pass(lgin2), lambda: gin(gin2))
            cols(node, mat["w2a"], ta[:, :], V["gin2_in"])
            pe.wait_ge(a_done, A["gin2_mid"])
            for c, n in CHUNKS:
                mm = pe.matmul(hid_ps[0:n, c:c + P], tb[:, c:c + n], mat["w2b"], start=True, stop=True)
            mm.then_inc(p_done, 1)

        @block.scalar
        def _(act):
            act.sem_inc(conv.hid_read, 1)
            for e in (lconv, lgin1, lgin2):
                act.sem_inc(e.part3, 1)
                act.sem_inc(e.stored, 2)
            act.sem_inc(hot_steps, 1)
            act.wait_ge(x_in, 16 * 2)
            for n, c in ((P, slice(0, WHOLE)), (REST, slice(WHOLE, WHOLE + 1))):
                act.activation(xy_row[0:n, c, :, 0, :], x_row[0:n, c, :, :], ACT.Copy)
            act.wait_ge(xy_made, 1)
            y_of = hid_ps.rearrange("p (c h f) -> p c h f", h=H, f=F)
            for n, c in ((P, slice(0, WHOLE)), (REST, slice(WHOLE, WHOLE + 1))):
                ins = act.activation(xy_row[0:n, c, :, 1, :], y_of[0:n, c, :, :], ACT.Copy)
            ins.then_inc(xy_ready, 1)
            learn_form(act)

            def silu_local(u, i, s, k):
                act.wait_ge(lconv.hid_made, 2 * u + k + 1)
                act.wait_ge(lconv.we_made[1], 2 * u + 1)
                act.activation(hid_sb[s][:, k, :], hid_ps, ACT.Silu, bias=b1_sb[:, 0:1]).then_inc(lconv.silu[s], 1)

            def store(e, u, i, s):
                act.wait_ge(e.summed_unit[s], i + 2)
                n = SPLITS * F + (1 if e.mlp else 0)
                act.activation(sums[:, bass.ds(u, 1), 0:n].rearrange("p o n -> p (o n)"), local_ps(e, s)[:, 0:n], ACT.Copy).then_inc(e.stored, 1)

            def local_pass(e):
                def part(n, u, i, s):
                    if n == 0:
                        act.wait_ge(e.values, u + 1)
                        if not e.mlp:
                            act.wait_ge(e.rows_in[s], 16 * e.by_dma * (i + 1))
                        act.wait_ge(e.summed_unit[s], i + 1)
                        value = rows[s][:, :, 0:F] if e.mlp else rows[s][:, :, F:2 * F]
                    else:
                        act.wait_ge((e.rest1, e.rest2)[n - 1], u + 1)
                        value = (rest1, rest2)[n - 1][:, :, :]
                    act.activation(parts[s][:, :, n * F:n * F + F], value, ACT.Copy).then_inc((e.part1, e.part2, e.part3)[n], 1)

                def source_distance(u, i, s):
                    act.wait_ge(e.l_in[s], 16 * (i + 1))
                    act.wait_ge(hot_steps, 2 * u + 1)
                    for c in range(WHOLE + 1):
                        ins = act.activation(distance[:, c, :], src_l_b[s][:, 0:e.onehot * P], ACT.Abs, scale=-1.0,
                                             bias=columns_sb[:, c:c + 1])
                    ins.then_inc(hot_steps, 1)

                def source_hots(u, i, s):
                    act.wait_ge(e.gathered[s], i + 1)
                    act.wait_ge(hot_steps, 2 * u + 2)
                    act.activation(src_hot[s][:, :, 0:e.onehot * P], distance[:, :, :], ACT.Relu, scale=-1.0,
                                   bias=col_one).then_inc(e.src_hots[s], 1)
                    act.wait_ge(e.src_hots[s], i + 1)
                    act.sem_inc(hot_steps, 1)

                def slot_distance(u):
                    if not is_first(u):
                        act.wait_ge(slot_hots, 2 * u)
                    act.activation(slot_tmp[:, :], iota_l[:, 0:REACH], ACT.Abs, bias=slot_neg[:, bass.ds(u, 1)]).then_inc(slot_hots, 1)

                def slot_onehot(u):
                    act.wait_ge(slot_hots, 2 * u + 1)
                    act.activation(slot_l[:, bass.ds(u, 1), :].rearrange("p o l -> p (o l)"), slot_tmp[:, :], ACT.Relu,
                                   scale=-1.0, bias=col_one).then_inc(slot_hots, 1)
                    act.activation(slot_hf[:, bass.ds(u, 1), :, :].rearrange("p o h f -> p (o h) f"),
                                   slot_h[:, bass.ds(u, 1), :].rearrange("p o h -> p (o h)").unsqueeze(2).to_broadcast([P, H, F]),
                                   ACT.Copy)

                def make_slot_part(n, h):
                    if n == 0:
                        act.wait_ge(slots_added, 2 * (e.halves + h) + 2)
                    else:
                        act.wait_ge(slot_left[n - 1], e.halves + h + 1)
                    act.activation(slot_parts[:, HALVES[h], n, :], (slot_v, slot_left1, slot_left2)[n][:, HALVES[h], :],
                                   ACT.Copy).then_inc(slot_part[n], 1)

                def gin_step(u, i, s, more):
                    if more == 0:
                        make_slot_part(0, 0)
                    part(0, u, i, s)
                    part(1, u, i, s)
                    part(2, u, i, s)
                    if not is_first(u):
                        store(e, *last_of(u, i, s))

                def conv_step(u, i, s, more):
                    if not is_first(u):
                        part(0, *last_of(u, i, s))
                        part(1, *last_of(u, i, s))
                    if more:
                        silu_local(*next_of(u, i, s), 1)
                    if more == 2:
                        source_distance(*second_of(u, i, s))
                    if not is_first(u):
                        part(2, *last_of(u, i, s))
                    if more == 2:
                        source_hots(*second_of(u, i, s))
                    slot_distance(u)
                    if more == 2:
                        silu_local(*second_of(u, i, s), 0)
                    slot_onehot(u)
                    if not is_first(u):
                        store(e, *last_of(u, i, s))

                if not e.mlp:
                    all_units(act, gin_step)
                else:
                    act.wait_ge(consts_in, 16 * CONSTANTS)
                    silu_local(0, 0, 0, 0)
                    source_distance(0, 0, 0)
                    source_hots(0, 0, 0)
                    silu_local(0, 0, 0, 1)
                    silu_local(1, 0, 1, 0)
                    source_distance(1, 0, 1)
                    source_hots(1, 0, 1)
                    act.wait_ge(consts_ready, 1)
                    all_units(act, conv_step)
                    part(0, UNITS - 1, UNITS // 2, 0)
                    part(1, UNITS - 1, UNITS // 2, 0)
                    make_slot_part(0, 0)
                    part(2, UNITS - 1, UNITS // 2, 0)
                make_slot_part(1, 0)
                store(e, UNITS - 1, UNITS // 2, 0)
                make_slot_part(2, 0)
                for n in range(SPLITS):
                    make_slot_part(n, 1)

            def silu(g, i, s):
                act.wait_ge(conv.hid_made, g + 1)
                act.wait_ge(conv.we_made[1][s], i + 1)
                act.activation(hid_sb[s][:, 0, :], hid_ps, ACT.Silu, bias=b1_sb[:, 0:1]).then_inc(conv.silu[s], 1)
                act.wait_ge(conv.silu[s], i + 1)
                act.sem_inc(conv.hid_read, 1)
            def general_conv():
                act.wait_ge(consts_in, 16 * CONSTANTS)
                pairs(act, silu)

            in_form(act, lambda: local_pass(lconv), general_conv)

            def one(v, dst, src, fn, **kw):
                act.wait_ge(v_done, v)
                act.activation(dst, src, fn, **kw).then_inc(a_done, 1)
            one(V["conv_var"], red2[:, :], red[:, :], ACT.Sqrt)
            one(V["conv_pre"], y2[:, :, :], y[:, :, :], ACT.Silu)
            one(V["res1_var"], red2[:, :], red[:, :], ACT.Sqrt)
            act.wait_ge(p_done, PD["x1_col"])
            act.activation(x1_col[:, :], node_ps[:, 0:L], ACT.Copy).then_inc(a_done, 1)
            in_form(act, lambda: local_pass(lgin1), lambda: act.nop())
            act.wait_ge(p_done, PD["gin1_a"])
            act.activation(tb[:, :], node_ps[:, 0:L], ACT.Relu, bias=vec["b1a"]).then_inc(a_done, 1)
            act.wait_ge(p_done, PD["gin1_b"])
            act.activation(h1_col[:, :], hid_ps[:, 0:L], ACT.Relu, bias=vec["b1b"]).then_inc(a_done, 1)
            in_form(act, lambda: local_pass(lgin2), lambda: act.nop())
            act.wait_ge(p_done, PD["gin2_a"])
            act.activation(tb[:, :], node_ps[:, 0:L], ACT.Relu, bias=vec["b2a"]).then_inc(a_done, 1)
            one(V["shifted"], y2[:, :, :], y[:, :, :], ACT.Exp)
            one(V["expsum"], red2[:, :], red[:, :], ACT.Ln)
            one(V["out_var"], red2[:, :], red[:, :], ACT.Sqrt)

        @block.vector
        def _(dve):
            state = {"v": 0}

            def done(ins, name=None):
                state["v"] += 1
                ins.then_inc(v_done, 1)
                if name:
                    assert V[name] == state["v"], (name, state["v"])

            def after():
                dve.wait_ge(v_done, state["v"])

            for e in (lconv, lgin1, lgin2):
                dve.sem_inc(e.rows_used, 2)
                for s in range(2):
                    dve.sem_inc(e.picks[s], 1)
            for q in range(2):
                dve.sem_inc(lconv.we_read[q], 1)

            steps = {"n": 0}

            def chain(ins):
                steps["n"] += 1
                ins.then_inc(setup, 1)

            def chained():
                dve.wait_ge(setup, steps["n"])

            dve.memset(x_row[:, WHOLE, :, :], 0.0).then_inc(zeroed, 1)
            dve.memset(zero_sb[:, :], 0.0)
            dve.memset(ones_sb[:, :], 1.0)
            dve.memset(one_row[:, :], 1.0)
            dve.memset(red[:, :], 1.0)
            dve.memset(b2_rows[:, :, :], 0.0)
            dve.memset(table_rest[:, :], 0.0)
            dve.memset(h1_row[:, WHOLE, :], 0.0)
            for s in range(2):
                dve.memset(parts[s][:, :, SPLITS * F:], 1.0)
            chain(dve.memset(y[:, :, :], 0.0))
            dve.wait_ge(ids_all_in, 16 * 3)
            chain(dve.tensor_tensor(local_dst[:, :, :], ids_all_sb[:, :, TILES:],
                                    bases_sb[:, :].unsqueeze(2).to_broadcast([P, GROUPS, TILES]), ALU.subtract))
            dve.wait_ge(slot_bases_in, 16 * 3)
            chain(dve.tensor_scalar(slot_n[:, :], slot_bases_sb[:, :], col_slot, None, ALU.add))
            chained()
            chain(dve.tensor_scalar(slot_ni[:, :], slot_n[:, :], H_BITS, None, ALU.logical_shift_right))
            dve.tensor_reduce(span[:, 0:1], local_dst[:, :, :], AX.XY, ALU.max)
            dve.tensor_reduce(span[:, 2:3], local_dst[:, :, :], AX.XY, ALU.min)
            chained()
            chain(dve.tensor_tensor(slot_rel[:, :], slot_ni[:, :], first_l[:, :], ALU.subtract))
            chained()
            dve.tensor_reduce(span[:, 1:2], slot_rel[:, :], AX.X, ALU.max)
            chain(dve.tensor_reduce(span[:, 3:4], slot_rel[:, :], AX.X, ALU.min))
            chained()
            dve.tensor_scalar(span[:, 0:2], span[:, 0:2], float(WINDOW), None, ALU.is_ge)
            chain(dve.tensor_scalar(span[:, 2:4], span[:, 2:4], 0.0, None, ALU.is_lt))
            chained()
            chain(dve.tensor_reduce(span[:, 4:5], span[:, 0:4], AX.X, ALU.add))
            assert SETUP_SPAN == steps["n"]
            dve.wait_ge(src_rows_in, 16)
            chain(dve.tensor_scalar(src_rows_sb[:, :], src_rows_sb[:, :], H_BITS, None, ALU.logical_shift_right))
            dve.wait_ge(span_sum, 1)
            dve.tensor_scalar(is_local[:, :], node_ps[0:1, 0:1], 0.0, None, ALU.is_equal).then_inc(form_known, 1)
            chained()
            dve.tensor_copy(src_l_rows[:, :], src_rows_sb[:, :]).then_inc(src_l_ready, 1)
            learn_form(dve)
            known = steps["n"]

            def prepare_b2():
                chain(dve.tensor_copy(b2_part[:, 0, :, :], b2_sb[:, :, :]))
                chained()
                chain(dve.tensor_tensor(b2_left[:, 0, :, :], b2_sb[:, :, :], b2_part[:, 0, :, :], ALU.subtract))
                chained()
                chain(dve.tensor_copy(b2_part[:, 1, :, :], b2_left[:, 0, :, :]))
                chained()
                chain(dve.tensor_tensor(b2_left[:, 1, :, :], b2_left[:, 0, :, :], b2_part[:, 1, :, :], ALU.subtract))
                chained()
                keep = [ident_sb[0:SPLITS, k:k + 1] for k in range(SPLITS)]
                chain(dve.tensor_scalar(b2_left[:, 1, :, :], b2_left[:, 1, :, :], keep[2], None, ALU.mult))
                for k in range(2):
                    chained()
                    ins = dve.scalar_tensor_tensor(b2_rows[0:SPLITS, :, :] if k else b2_left[:, 1, :, :], b2_part[:, k, :, :], keep[k],
                                                   b2_left[:, 1, :, :], ALU.mult, ALU.add)
                    if k == 0:
                        chain(ins)
                ins.then_inc(consts_ready, 1)

            def prepare_general():
                steps["n"] = known
                dve.wait_ge(consts_in, 16 * CONSTANTS)
                prepare_b2()

            def prepare_local():
                steps["n"] = known
                dve.wait_ge(consts_in, 16 * CONSTANTS)
                chain(dve.tensor_scalar(src_h_sb[:, :, :], ids_all_sb[:, :, 0:TILES], H - 1, None, ALU.bitwise_and))
                dve.tensor_copy(local16[:, :, :].rearrange("p u t -> p (u t)"), local_dst[:, :, :].rearrange("p g t -> p (g t)"))
                chain(dve.tensor_scalar(slot_n[:, :], slot_n[:, :], H - 1, None, ALU.bitwise_and))
                chained()
                dve.tensor_tensor(slot_h[:, :, :], slot_n[:, :].unsqueeze(2).to_broadcast([P, UNITS, H]),
                                  iota_h.unsqueeze(1).to_broadcast([P, UNITS, H]), ALU.is_equal)
                chain(dve.tensor_scalar(slot_neg[:, :], slot_rel[:, :], -1.0, None, ALU.mult))
                prepare_b2()
                chain(dve.tensor_tensor(masks[:, :, :, :],
                                  src_h_sb[:, :, :].rearrange("p g t -> p (g t)").rearrange("p (u t) -> p u t", t=UNIT)[:, :, DMA_GIN:]
                                  .unsqueeze(3).to_broadcast([P, UNITS, ONEHOT, H]),
                                  iota_h.unsqueeze(1).unsqueeze(1).to_broadcast([P, UNITS, ONEHOT, H]), ALU.is_equal))
                chained()

            def build_table(e, source):
                whole = source.rearrange("p c n -> p (c n)").rearrange("p (c n) -> p c n", n=P)
                left = picked[:, 0:4, :, :].rearrange("p c h f -> p c (h f)")
                at = {"n": 0}

                def part_chain(ins):
                    at["n"] += 1
                    ins.then_inc(e.table_steps, 1)
                    dve.wait_ge(e.table_steps, at["n"])
                part_chain(dve.tensor_copy(table_parts[:, :, 0, :], whole))
                part_chain(dve.tensor_tensor(left, whole, table_parts[:, :, 0, :], ALU.subtract))
                part_chain(dve.tensor_copy(table_parts[:, :, 1, :], left))
                part_chain(dve.tensor_tensor(left, left, table_parts[:, :, 1, :], ALU.subtract))
                dve.tensor_copy(table_parts[:, :, 2, :], left).then_inc(e.table, 1)

            def source_hots(e, u, i, s, chunks):
                n = e.onehot * P
                for c in chunks:
                    if c == 0:
                        dve.wait_ge(e.l_in[s], 16 * (i + 1))
                        dve.wait_ge(e.gathered[s], i + 1)
                    ins = dve.tensor_scalar(src_hot[s][:, c, 0:n], src_l_b[s][:, 0:n], columns_sb[:, c:c + 1], None, ALU.is_equal)
                    if c == WHOLE:
                        ins.then_inc(e.src_hots[s], 1)

            def dest_hots(e, u, i, s):
                dve.wait_ge(e.summed_unit[s], i + 1)
                dve.tensor_tensor(dst_hot[s][:, :, :], slot_iota_sb[:, :].rearrange("p (w t) -> p w t", t=UNIT),
                                  local16[:, bass.ds(u, 1), :].to_broadcast([P, WINDOW, UNIT]), ALU.is_equal).then_inc(e.dst_hots, 1)

            def local_pass(e, source):
                build_table(e, source)
                if e.mlp:
                    prepare_local()
                else:
                    for s in range(2):
                        source_hots(e, s, 0, s, range(WHOLE + 1))

                def choose(u, i, s):
                    dve.wait_ge(e.gathered[s], i + 2)
                    first = gather_bank(e, s)
                    cols_g = bank[:, first:first + -(-e.onehot // 4), :].rearrange("p b n -> p (b n)")[:, 0:e.onehot * P].rearrange(
                        "p (t h f) -> p t h f", h=H, f=F)
                    mid = e.onehot // 2
                    for k, (a, b) in enumerate(((0, mid), (mid, e.onehot))):
                        mask = masks[:, bass.ds(u, 1), ONEHOT - e.onehot + a:ONEHOT - e.onehot + b, :].rearrange(
                            "p o t h -> p (o t) h").unsqueeze(3).to_broadcast([P, b - a, H, F])
                        dve.tensor_tensor(picked[:, a:b, :, :], cols_g[:, a:b, :, :], mask,
                                          ALU.mult).then_inc(e.chain if k == 0 else e.picks[s], 1)
                    for k, (a, b) in enumerate(((0, mid), (mid, e.onehot))):
                        if k == 0:
                            dve.wait_ge(e.chain, u + 1)
                        else:
                            dve.wait_ge(e.picks[s], i + 2)
                        ins = dve.tensor_reduce(rows[s][:, e.by_dma + a:e.by_dma + b, F:2 * F],
                                                picked[:, a:b, :, :].rearrange("p t h f -> p t f h"), AX.X, ALU.add)
                    ins.then_inc(e.chosen if e.mlp else e.values, 1)

                def leave1(u, i, s):
                    dve.wait_ge(e.part1, u + 1)
                    value = rows[s][:, :, 0:F] if e.mlp else rows[s][:, :, F:2 * F]
                    dve.tensor_tensor(rest1[:, :, :], value, parts[s][:, :, 0:F], ALU.subtract).then_inc(e.rest1, 1)

                def leave2(u, i, s):
                    dve.wait_ge(e.part2, u + 1)
                    dve.wait_ge(e.rest1, u + 1)
                    if not e.mlp:
                        dve.sem_inc(e.rows_used, 1)
                    dve.wait_ge(e.part3, u + 1)
                    dve.tensor_tensor(rest2[:, :, :], rest1[:, :, :], parts[s][:, :, F:2 * F], ALU.subtract).then_inc(e.rest2, 1)

                def add_up(h):
                    half = HALVES[h]
                    dve.wait_ge(e.stored, 2 + half.stop)
                    dve.tensor_tensor(slot_v[:, half, :], sums[:, half, 0:F], sums[:, half, F:2 * F], ALU.add).then_inc(slots_added, 1)
                    dve.wait_ge(slots_added, 2 * (e.halves + h) + 1)
                    dve.tensor_tensor(slot_v[:, half, :], slot_v[:, half, :], sums[:, half, 2 * F:3 * F], ALU.add).then_inc(slots_added, 1)

                def slot_leave1(h):
                    half = HALVES[h]
                    dve.wait_ge(slot_part[0], e.halves + h + 1)
                    dve.tensor_tensor(slot_left1[:, half, :], slot_v[:, half, :], slot_parts[:, half, 0, :],
                                      ALU.subtract).then_inc(slot_left[0], 1)

                def slot_leave2(h):
                    half = HALVES[h]
                    dve.wait_ge(slot_part[1], e.halves + h + 1)
                    dve.wait_ge(slot_left[0], e.halves + h + 1)
                    dve.tensor_tensor(slot_left2[:, half, :], slot_left1[:, half, :], slot_parts[:, half, 1, :],
                                      ALU.subtract).then_inc(slot_left[1], 1)

                def spread_turn(t, i, b):
                    dve.wait_ge(e.spreads_used[b], i + 1)
                    units = slice(TURN * t, TURN * t + TURN) if isinstance(t, int) else bass.ds(TURN * t, TURN)
                    dve.tensor_tensor(slot_spread[b][:, :, :, :, :],
                                      slot_parts[:, units, :, :].unsqueeze(3).to_broadcast([P, TURN, SPLITS, H, F]),
                                      slot_hf[:, units, :, :].unsqueeze(2).to_broadcast([P, TURN, SPLITS, H, F]),
                                      ALU.mult).then_inc(e.spreads[b], 1)

                def gin_step(u, i, s, more):
                    choose(u, i, s)
                    dest_hots(e, u, i, s)
                    if more == 2:
                        source_hots(e, *second_of(u, i, s), (0, 1))
                    if more == 0:
                        add_up(0)
                    leave1(u, i, s)
                    if more == 2:
                        source_hots(e, *second_of(u, i, s), (2, 3))
                    leave2(u, i, s)

                def conv_step(u, i, s, more):
                    def product(q):
                        dve.wait_ge(e.we_made[q % 2], 2 * u + q // 2 + 1 + 3 * (q % 2))
                        if q >= 2:
                            dve.wait_ge(e.reduced, 3 * u + q - 1)
                        elif not is_first(u):
                            dve.wait_ge(e.values if q else e.reduced, u if q else 3 * u)
                        weights = bank[:, 3 + 2 * (q % 2):5 + 2 * (q % 2), :].rearrange("p b (k o i) -> p (b k) o i", k=2, o=F)
                        x_in_edge = rows[s][:, 4 * q:4 * q + 4, F:2 * F].unsqueeze(2).to_broadcast([P, 4, F, F])
                        dve.tensor_tensor(prod[q % 2][:, :, :, :], weights, x_in_edge, ALU.mult).then_inc(e.we_read[q % 2], 1)

                    def reduction(q):
                        dve.wait_ge(e.we_read[q % 2], 2 * u + q // 2 + 2)
                        ins = dve.tensor_reduce(rows[s][:, 4 * q:4 * q + 4, 0:F], prod[q % 2][:, :, :, :], AX.X, ALU.add)
                        ins.then_inc(e.reduced if q < 3 else e.values, 1)

                    choose(u, i, s)
                    dve.wait_ge(e.rows_in[s], 16 * e.by_dma * (i + 1))
                    product(0)
                    if not is_first(u):
                        leave1(*last_of(u, i, s))
                    product(1)
                    reduction(0)
                    if not is_first(u):
                        leave2(*last_of(u, i, s))
                    dest_hots(e, u, i, s)
                    product(2)
                    reduction(1)
                    dve.wait_ge(e.chosen, u + 1)
                    product(3)
                    reduction(2)
                    dve.wait_ge(e.reduced, 3 * u + 3)
                    dve.tensor_tensor(rows[s][:, 0:e.by_dma, 0:F], rows[s][:, 0:e.by_dma, 0:F],
                                      rows[s][:, 0:e.by_dma, 2 * F:3 * F], ALU.add).then_inc(e.rows_used, 1)
                    reduction(3)

                if e.mlp:
                    all_units(dve, conv_step)
                    leave1(UNITS - 1, UNITS // 2, 0)
                    add_up(0)
                    leave2(UNITS - 1, UNITS // 2, 0)
                else:
                    all_units(dve, gin_step)
                slot_leave1(0)
                slot_leave2(0)
                dve.wait_ge(slot_part[2], e.halves + 1)
                early = HALVES[0].stop // TURN // AHEAD * AHEAD
                spread_turn(0, 0, 0)
                spread_turn(1, 0, 1)
                add_up(1)
                if e.mlp:
                    dve.tensor_tensor(slot_cnt[:, :, :], slot_h[:, :, :],
                                      sums[:, :, SPLITS * F:SPLITS * F + 1].to_broadcast([P, UNITS, H]), ALU.mult).then_inc(slot_cnt_made, 1)
                spread_turn(2, 0, 2)
                slot_leave1(1)
                spread_turn(3, 0, 3)
                slot_leave2(1)
                for t in range(AHEAD, early):
                    spread_turn(t, t // AHEAD, t % AHEAD)
                dve.wait_ge(slot_part[2], e.halves + 2)
                all_turns(dve, spread_turn, first=early // AHEAD)
                dve.wait_ge(e.summed, 1)

            def edge_pass(e):
                per = 9 if e.mlp else 7
                left1, left2 = rest1[:, 0:TILES, :], rest2[:, 0:TILES, :]

                def step(g, i, s):
                    at = {"n": 0}

                    def chain(ins):
                        at["n"] += 1
                        ins.then_inc(e.vec, 1)

                    def chained(back=0):
                        dve.wait_ge(e.vec, per * g + at["n"] - back)

                    dve.wait_ge(e.ids_in[s], 16 * (i + 1))
                    dve.wait_ge(e.scattered[s], i + 1)
                    dve.tensor_scalar(dst_h[:, :], ids_sb[s][:, 0, TILES:], H - 1, None, ALU.bitwise_and)
                    chain(dve.tensor_scalar(dst_l[:, :], ids_sb[s][:, 0, TILES:], H_BITS, None, ALU.logical_shift_right))
                    chained()
                    dve.tensor_copy(dst_hf[:, :], dst_h[:, :])
                    chain(dve.tensor_copy(dst_lf[:, :], dst_l[:, :]))
                    chained()
                    dve.tensor_tensor(hot_h[s][:, :, :], dst_hf[:, :].unsqueeze(2).to_broadcast([P, TILES, H]),
                                      iota_h.unsqueeze(1).to_broadcast([P, TILES, H]), ALU.is_equal).then_inc(e.ids_used[s], 1)
                    for t in range(TILES):
                        ins = dve.tensor_scalar(hot_l[s][:, t, :], iota_l[:, :], dst_lf[:, t:t + 1], None, ALU.is_equal)
                    ins.then_inc(e.hots[s], 1)
                    dve.wait_ge(e.rows_in[s], 16 * TILES * (i + 1))
                    if e.mlp:
                        for q in range(2):
                            dve.wait_ge(e.we_made[q][s], i + 2)
                            weights = we_ps[:, 2 * q:2 * q + 2, :].rearrange("p b (k o i) -> p (b k) o i", k=2, o=F)
                            x_in_edge = rows[s][:, 4 * q:4 * q + 4, F:2 * F].unsqueeze(2).to_broadcast([P, 4, F, F])
                            dve.tensor_tensor(prod[q][:, :, :, :], weights, x_in_edge, ALU.mult).then_inc(e.we_read[q], 1)
                            dve.wait_ge(e.we_read[q], g + 2)
                            chain(dve.tensor_reduce(msg[:, 4 * q:4 * q + 4, :], prod[q][:, :, :, :], AX.X, ALU.add))
                        chained()
                        dve.sem_inc(e.rows_used[s], 1)
                        value = msg[:, :, :]
                    else:
                        value = rows[s][:, 0:TILES, F:2 * F]
                    chain(dve.tensor_copy(part[0][:, :, :], value))
                    chained()
                    chain(dve.tensor_tensor(left1, value, part[0][:, :, :], ALU.subtract))
                    chained()
                    if not e.mlp:
                        dve.sem_inc(e.rows_used[s], 1)
                    chain(dve.tensor_copy(part[1][:, :, :], left1))
                    chained()
                    chain(dve.tensor_tensor(left2, left1, part[1][:, :, :], ALU.subtract))
                    chained()
                    chain(dve.tensor_copy(part[2][:, :, :], left2))
                    chained()
                    for k in range(SPLITS):
                        ins = dve.tensor_tensor(spread[s][:, k, :, :, :],
                                                part[k][:, :, :].unsqueeze(2).to_broadcast([P, TILES, H, F]),
                                                hot_h[s][:, :, :].unsqueeze(3).to_broadcast([P, TILES, H, F]), ALU.mult)
                    ins.then_inc(e.spreads[s], 1)
                    assert at["n"] == per

                pairs(dve, step)
                dve.wait_ge(e.summed, 1)

            def per_node(col):
                return col[:, :].unsqueeze(2).to_broadcast([P, 4 * H, F])

            def normed(var_name, sqrt_at, out_rows, last):
                done(dve.tensor_reduce(red[:, :], y[:, :, :], AX.X, ALU.add))
                after()
                done(dve.tensor_scalar(red[:, :], red[:, :], 1.0 / F, None, ALU.mult))
                after()
                done(dve.tensor_tensor(y[:, :, :], y[:, :, :], per_node(red), ALU.subtract))
                after()
                done(dve.tensor_tensor(y2[:, :, :], y[:, :, :], y[:, :, :], ALU.mult))
                after()
                done(dve.tensor_reduce(red[:, :], y2[:, :, :], AX.X, ALU.add))
                after()
                done(dve.tensor_scalar(red[:, :], red[:, :], 1.0 / F, EPS, ALU.mult, ALU.add), var_name)
                dve.wait_ge(a_done, sqrt_at)
                done(dve.reciprocal(red[:, :], red2[:, :]))
                after()
                done(dve.tensor_tensor(out_rows, y[:, :, :], per_node(red), ALU.mult), last)
                after()

            def general_conv():
                prepare_general()
                edge_pass(conv)

            dve.wait_ge(x_in, 16 * 2)
            in_form(dve, lambda: local_pass(lconv, x_row[:, :, :, :].rearrange("p c h f -> p c (h f)")), general_conv)
            done(dve.tensor_copy(tb[:, :], acc))
            done(dve.tensor_scalar(edges_in[:, :], cnt[0:H, :], 1.0, None, ALU.max), "edges_in")
            dve.wait_ge(p_done, PD["rows"])
            blocks = ((P, slice(0, H * WHOLE)), (REST, slice(H * WHOLE, H * WHOLE + H)))
            by_node = {name: ps_rows.rearrange("p (n f) -> p n f", f=F) for name, ps_rows in (("sums", node_ps), ("root", hid_ps))}
            for n, at in blocks:
                done(dve.reciprocal(red[0:n, at], bank[0:n, 3, at]))
            after()
            for n, at in blocks:
                done(dve.tensor_tensor(y[0:n, at, :], by_node["sums"][0:n, at, :],
                                       red[0:n, at].unsqueeze(2).to_broadcast([n, at.stop - at.start, F]), ALU.mult))
            after()
            for n, at in blocks:
                done(dve.tensor_tensor(y[0:n, at, :], y[0:n, at, :], by_node["root"][0:n, at, :], ALU.add))
            after()
            normed("conv_var", A["conv_sqrt"], y[:, :, :], None)

            def rows_of(rows):
                return rows.unsqueeze(1).to_broadcast([P, 4, H, F])

            y_rows, x_nodes = y[:, :, :].rearrange("p (c h) f -> p c h f", h=H), x_row[:, :, :, :].rearrange("p c h f -> p (c h) f")
            x1_nodes = x1_row[:, :, :].rearrange("p c (h f) -> p (c h) f", f=F)
            done(dve.tensor_tensor(y_rows, y_rows, rows_of(row_vec["ln_w"]), ALU.mult))
            after()
            done(dve.tensor_tensor(y_rows, y_rows, rows_of(row_vec["ln_b"]), ALU.add))
            after()
            done(dve.tensor_tensor(y[:, :, :], y[:, :, :], x_nodes, ALU.add), "conv_pre")
            dve.wait_ge(a_done, A["conv_silu"])
            done(dve.tensor_tensor(y[:, :, :], y2[:, :, :], x_nodes, ALU.add))
            after()
            normed("res1_var", A["res1_sqrt"], x1_nodes, "x1_row")

            in_form(dve, lambda: local_pass(lgin1, x1_row[:, :, :]), lambda: edge_pass(gin1))
            dve.wait_ge(a_done, A["x1_col"])
            done(dve.tensor_scalar(tb[:, :], x1_col[:, :], vec["eps1"], None, ALU.mult))
            after()
            done(dve.tensor_tensor(tb[:, :], tb[:, :], x1_col[:, :], ALU.add))
            after()
            done(dve.tensor_tensor(ta[:, :], tb[:, :], acc, ALU.add), "gin1_in")
            dve.wait_ge(p_done, PD["h1_row"])
            for c, n in CHUNKS:
                done(dve.tensor_copy(h1_row[0:n, c // P, :], node_ps[0:n, c:c + P]), "h1_row" if n < P else None)

            after()
            in_form(dve, lambda: local_pass(lgin2, h1_row[:, :, :]), lambda: edge_pass(gin2))
            done(dve.tensor_scalar(tb[:, :], h1_col[:, :], vec["eps2"], None, ALU.mult))
            after()
            done(dve.tensor_tensor(tb[:, :], tb[:, :], h1_col[:, :], ALU.add))
            after()
            done(dve.tensor_tensor(ta[:, :], tb[:, :], acc, ALU.add), "gin2_in")
            dve.wait_ge(p_done, PD["logits"])
            for c, n in CHUNKS:
                done(dve.tensor_tensor(y[0:n, 8 * (c // P):8 * (c // P) + 8, :],
                                       hid_ps[0:n, c:c + P].rearrange("p (h f) -> p h f", f=F),
                                       row_vec["b2b"][0:n, :, :], ALU.add))
            after()
            done(dve.tensor_reduce(red[:, :], y[:, :, :], AX.X, ALU.max))
            after()
            done(dve.tensor_tensor(y[:, :, :], y[:, :, :], per_node(red), ALU.subtract), "shifted")
            dve.wait_ge(a_done, A["exp"])
            done(dve.tensor_reduce(red[:, :], y2[:, :, :], AX.X, ALU.add), "expsum")
            dve.wait_ge(a_done, A["ln"])
            done(dve.tensor_tensor(y[:, :, :], y[:, :, :], per_node(red2), ALU.subtract))
            after()
            done(dve.tensor_tensor(y[:, :, :], y[:, :, :], x1_nodes, ALU.add))
            after()
            normed("out_var", A["sqrt"], y[:, :, :], "out")


SETUP_SPAN = 8
V = {"edges_in": 2, "conv_var": 14, "conv_pre": 19, "res1_var": 26, "x1_row": 28, "gin1_in": 31, "h1_row": 35,
     "gin2_in": 38, "shifted": 44, "expsum": 45, "out_var": 53, "out": 55}
A = {"conv_sqrt": 1, "conv_silu": 2, "res1_sqrt": 3, "x1_col": 4, "gin1_mid": 5, "h1": 6, "gin2_mid": 7, "exp": 8,
     "ln": 9, "sqrt": 10}
PD = {"root": 1, "rows": 2, "x1_col": 3, "gin1_a": 4, "gin1_b": 5, "h1_row": 6, "gin2_a": 7, "logits": 8}


def kernel(**inputs):
    import numpy as np
    import concourse.bacc as bacc
    from concourse.bass_utils import run_bass_kernel_spmd

    a = {k: np.asarray(v) for k, v in inputs.items()}
    f32 = np.float32

    x_pad = np.zeros((L * H, F), f32)
    x_pad[:NODES] = a["x"]
    x_rows = x_pad.reshape(L, P)

    slots = GROUPS * TILES * P
    src = np.zeros(slots, np.int32)
    dst = np.full(slots, NODES, np.int32)
    src[:EDGES], dst[:EDGES] = a["src"], a["dst"]
    ids = np.concatenate([v.reshape(GROUPS, TILES, P).transpose(0, 2, 1) for v in (src, dst)], axis=2)

    ids_all = ids.transpose(1, 0, 2)
    bases = dst[::TILES * P].reshape(1, GROUPS)
    slot_bases = bases.reshape(UNITS, 2).T
    first_cols = (TURN_L * (np.arange(UNITS) // TURN) - MARGIN).astype(f32).reshape(1, UNITS)
    p = np.arange(P)
    columns = np.full((P, WHOLE + 3), -1.0, f32)
    for c in range(WHOLE):
        columns[:, c] = c * P + p
    columns[:SPLITS * REST, WHOLE] = WHOLE * P + p[:SPLITS * REST] % REST
    columns[:, WHOLE + 1], columns[:, WHOLE + 2] = p % WINDOW, 1.0

    attr = np.zeros((slots, EDGE_F), f32)
    attr[:EDGES] = a["edge_attr_8"]
    attr = attr.reshape(GROUPS, 2, 2, 2, P, EDGE_F).transpose(0, 3, 5, 1, 2, 4).reshape(GROUPS, 2 * EDGE_F, 4 * P)

    def diagonal(w, n):
        out = np.zeros((n * w.shape[0], n * w.shape[1]), f32)
        for k in range(n):
            out[k * w.shape[0]:(k + 1) * w.shape[0], k * w.shape[1]:(k + 1) * w.shape[1]] = w
        return out

    w1 = diagonal(a["L0_gnn_W1"], 2)
    b1 = np.tile(a["L0_gnn_b1"], 2).reshape(P, 1)
    w2 = a["L0_gnn_W2"].reshape(HIDDEN, F, F).transpose(0, 2, 1).reshape(HIDDEN, F * F)
    w2 = diagonal(w2, 2)
    b2 = np.broadcast_to(a["L0_gnn_b2"].reshape(F, F).T.reshape(1, 1, F * F), (SPLITS, 2, F * F))
    mats = {"root": a["L0_gnn_root"], "w1a": a["L1_gnn_w1a"],
            "w1b": a["L1_gnn_w1b"], "w2a": a["L1_gnn_w2a"], "w2b": a["L1_gnn_w2b"]}
    row_vecs = {"bias": a["L0_gnn_bias"], "ln_w": a["L0_gnn_ln_w"], "ln_b": a["L0_gnn_ln_b"], "b2b": a["L1_gnn_b2b"]}
    row_vecs = np.stack([np.tile(row_vecs[n], H) for n in ROWS]).reshape(1, len(ROWS), H, F)
    vecs = {"b1a": a["L1_gnn_b1a"],
            "b1b": a["L1_gnn_b1b"], "b2a": a["L1_gnn_b2a"], "eps1": np.full(F, a["L1_gnn_eps1"]),
            "eps2": np.full(F, a["L1_gnn_eps2"])}
    arrays = {
        "x_rows": x_rows, "x_cols": x_rows.T, "ids": ids, "ids_all": ids_all,
        "src_rows": src.reshape(GROUPS, TILES * P), "bases": bases, "slot_bases": slot_bases, "first_cols": first_cols,
        "edge_attr": attr, "w1": w1, "b1": b1, "w2": w2, "b2": b2,
        "b2_mat": diagonal(a["L0_gnn_b2"].reshape(F, F), H),
        "mats": np.stack([diagonal(mats[n], H) for n in MATS], axis=1),
        "vecs": np.stack([np.tile(vecs[n], H) for n in VECS], axis=1),
        "row_vecs": np.broadcast_to(row_vecs, (P, len(ROWS), H, F)),
        "ident": np.eye(P, dtype=f32),
        "iota_cols": np.broadcast_to(np.arange(LP).astype(np.float16), (P, LP)),
        "slot_iota": np.broadcast_to(np.repeat(np.arange(WINDOW), UNIT).astype(np.float16), (P, WINDOW * UNIT)),
        "columns": columns,
    }
    arrays = {k: np.ascontiguousarray(v) for k, v in arrays.items()}
    nc = bacc.Bacc("TRN2", target_bir_lowering=False, num_devices=1)
    args = [nc.dram_tensor(f"in_{k}", v.shape, mybir.dt.from_np(v.dtype), kind="ExternalInput").ap()
            for k, v in arrays.items()]
    out = nc.dram_tensor("out_0", (NODES, F), mybir.dt.float32, kind="ExternalOutput").ap()
    gnn_kernel(nc, *args, out)
    r = run_bass_kernel_spmd(nc, [{f"in_{k}": v for k, v in arrays.items()}], core_ids=[0])
    return r.results[0]["out_0"]
```
